# Optimizing a Trainium2 kernel written in Bass

```python
import numpy as np
import jax
import jax.numpy as jnp

def _softmax(x, axis=-1):
    return jax.nn.softmax(x, axis=axis)

def _gelu(x):
    return jax.nn.gelu(x, approximate=True)

def _silu(x):
    return jax.nn.silu(x)

def _sigmoid(x):
    return jax.nn.sigmoid(x)

def _layernorm(x, axis=-1, eps=1e-05):
    m = jnp.mean(x, axis=axis, keepdims=True)
    v = jnp.var(x, axis=axis, keepdims=True)
    return (x - m) / jnp.sqrt(v + eps)

def _scatter_add(tgt, idx, src, axis=0):
    return tgt.at[idx].add(src)

def _segment_sum(src, seg, n):
    return jax.ops.segment_sum(src, seg, n)
kernel_name = 'mk_seq_postln_d1_jaxref_r2_eff1e5'

def setup_inputs(seed: int=0):
    np.random.seed(seed)
    _w = jnp.asarray

    def _L0_attn_setup():
        import jax, jax.numpy as jnp
        import numpy as np
        import math
        NUM_RFS = 512
        DIM = 512
        OUT_DIM = 512
        B, S = (4, 1024)

        def _rfs(xw, ab, AB, gs):
            dot_products = jnp.einsum('...d,rd->...r', xw, ab[:, None] * gs)
            correction = (0.5 * jnp.sum(xw * xw, axis=-1))[..., None] * (ab * ab)
            return 1.0 / math.sqrt(NUM_RFS) * AB * jnp.exp(dot_products - correction)
        key = jax.random.key(seed)
        k1, k2, k3, k4 = jax.random.split(key, 4)
        x = jax.random.normal(k1, (B, S, DIM), dtype=jnp.float32) * 0.03
        input_weights = jax.random.normal(k2, (OUT_DIM, DIM), dtype=jnp.float32) * 0.03
        xis = jax.random.uniform(k3, (NUM_RFS,), dtype=jnp.float32) * 0.5
        proj_matrix = jax.random.normal(k4, (NUM_RFS, DIM), dtype=jnp.float32)
        return {'x': x, 'input_weights': input_weights, 'xis': xis, 'proj_matrix': proj_matrix}
    _L0_attn_in = _L0_attn_setup()

    def _L0_ffn_setup():
        import jax, jax.numpy as jnp
        import numpy as np
        INPUT_SIZE = 512
        OUTPUT_SIZE = 512
        key = jax.random.key(seed)
        kx, kt, kp, ktn, kpn = jax.random.split(key, 5)
        x = jax.random.normal(kx, (8, 1024, INPUT_SIZE), dtype=jnp.float32)
        theta = jax.random.normal(kt, (INPUT_SIZE, OUTPUT_SIZE), dtype=jnp.float32) * 0.02
        phi = jax.random.normal(kp, (INPUT_SIZE, OUTPUT_SIZE), dtype=jnp.float32) * 0.02
        theta_noise = jax.random.normal(ktn, (INPUT_SIZE, OUTPUT_SIZE), dtype=jnp.float32) * 0.01
        phi_noise = jax.random.normal(kpn, (INPUT_SIZE, OUTPUT_SIZE), dtype=jnp.float32) * 0.01
        return {'x': x, 'theta': theta, 'phi': phi, 'theta_noise': theta_noise, 'phi_noise': phi_noise}
    _L0_ffn_in = _L0_ffn_setup()
    _d = {'L0_attn_x': _L0_attn_in['x'], 'L0_attn_input_weights': _L0_attn_in['input_weights'], 'L0_attn_xis': _L0_attn_in['xis'], 'L0_attn_proj_matrix': _L0_attn_in['proj_matrix'], 'L0_ffn_theta': _L0_ffn_in['theta'], 'L0_ffn_phi': _L0_ffn_in['phi'], 'L0_ffn_theta_noise': _L0_ffn_in['theta_noise'], 'L0_ffn_phi_noise': _L0_ffn_in['phi_noise']}
    _x0 = _d['L0_attn_x']
    _d['L0_attn_x'] = jax.random.normal(jax.random.fold_in(jax.random.key(seed), 1), (4, 2048, 512), dtype=_x0.dtype)
    del _x0
    return _d

def reference(L0_attn_x, L0_attn_input_weights, L0_attn_xis, L0_attn_proj_matrix, L0_ffn_theta, L0_ffn_phi, L0_ffn_theta_noise, L0_ffn_phi_noise):

    def _L0_attn_ref(x, input_weights, xis, proj_matrix):
        import jax, jax.numpy as jnp
        import numpy as np
        import math
        NUM_RFS = 512
        DIM = 512
        OUT_DIM = 512
        B, S = (4, 1024)

        def _rfs(xw, ab, AB, gs):
            dot_products = jnp.einsum('...d,rd->...r', xw, ab[:, None] * gs)
            correction = (0.5 * jnp.sum(xw * xw, axis=-1))[..., None] * (ab * ab)
            return 1.0 / math.sqrt(NUM_RFS) * AB * jnp.exp(dot_products - correction)
        ab = xis
        AB = jnp.exp(xis)
        weights = _rfs(input_weights, ab, AB, proj_matrix)
        feats = _rfs(x, ab, AB, proj_matrix)
        return jnp.einsum('bsr,or->bso', feats, weights)

    def _L0_ffn_ref(x, theta, phi, theta_noise, phi_noise):
        import jax, jax.numpy as jnp
        import numpy as np
        INPUT_SIZE = 512
        OUTPUT_SIZE = 512
        real = jnp.einsum('bti,io->bto', x, jnp.cos(theta + theta_noise))
        imag = jnp.einsum('bti,io->bto', x, jnp.sin(phi + phi_noise))
        return jnp.sqrt(real * real + imag * imag)
    x = L0_attn_x
    x = _layernorm(x + _L0_attn_ref(x, L0_attn_input_weights, L0_attn_xis, L0_attn_proj_matrix), axis=-1)
    x = _layernorm(x + _L0_ffn_ref(x, L0_ffn_theta, L0_ffn_phi, L0_ffn_theta_noise, L0_ffn_phi_noise), axis=-1)
    return x

_drawn_inputs = setup_inputs


def setup_inputs(seed=0):
    import zlib

    import numpy as np

    out = dict(_drawn_inputs(seed))
    spreads = {}
    factors = {'L0_ffn_theta': 8.0, 'L0_ffn_theta_noise': 8.0}
    for name, (base, spread) in spreads.items():
        noise = np.random.default_rng([zlib.crc32(name.encode()), seed]).standard_normal(out[name].shape)
        drawn = base * np.exp(spread * noise) if base else spread * noise
        out[name] = jnp.asarray(drawn.astype(out[name].dtype))
    for name, factor in factors.items():
        out[name] = (out[name] * factor).astype(out[name].dtype)
    return out
```

```python
from contextlib import ExitStack

import numpy as np

import concourse.bass as bass
from concourse import mybir

P = 128
ALU = mybir.AluOpType
ACT = mybir.ActivationFunctionType
F32 = mybir.dt.float32
F32R = mybir.dt.float32r

EPS = 1e-5
TWO_PI_A = 6.28125
TWO_PI_B = float(np.float32(np.round((2 * np.pi - TWO_PI_A) * 2**22) / 2**22))
TWO_PI_C = float(np.float32(2 * np.pi - TWO_PI_A - TWO_PI_B))
ROUNDER = 1.5 * 2.0**23
PI_INSIDE = float(np.nextafter(np.float32(np.pi), np.float32(0)))
HALF_PI = float(np.float32(np.pi / 2))


def build(nc, xT, x, wT, w, xis, gsT, theta, phi, theta_noise, phi_noise, out):
    T, D = x.shape
    R = gsT.shape[1]
    O = w.shape[0]
    B = 512
    NB = T // B
    C = D // P
    assert D == R == O == B == C * P and T % (2 * B) == 0 and NB >= 4

    xT_blocks = xT.rearrange("(c p) (b t) -> b p c t", p=P, t=B)
    x_blocks = x.rearrange("(b c p) d -> b p c d", p=P, c=C)
    out_tiles = out.rearrange("(b c p) d -> b c p d", p=P, c=C)
    by_chunk = lambda m: m.rearrange("(c p) n -> p c n", p=P)
    norms_dram = nc.dram_tensor("token_norms", (B,), F32, kind="Internal").ap()

    with ExitStack() as ctx:
        sb = lambda name, shape, dt=F32: ctx.enter_context(nc.sbuf_tensor(name, shape, dt))
        bank = lambda name: ctx.enter_context(nc.psum_tensor(name, [P, 512], F32))
        sem = lambda name: ctx.enter_context(nc.semaphore(name))

        gs_hi, gs_lo = sb("gs_hi", [P, C, R], F32R), sb("gs_lo", [P, C, R], F32R)
        W_hi, W_lo = sb("W_hi", [P, C, O], F32R), sb("W_lo", [P, C, O], F32R)
        cos_hi, cos_lo = sb("cos_hi", [P, C, O], F32R), sb("cos_lo", [P, C, O], F32R)
        sin_hi, sin_lo = sb("sin_hi", [P, C, O], F32R), sb("sin_lo", [P, C, O], F32R)
        xT_raw = sb("xT_raw", [P, C, B])
        xT_hi, xT_lo = sb("xT_hi", [P, C, B], F32R), sb("xT_lo", [P, C, B], F32R)
        x_tok = sb("x_tok", [P, 2, C, D])
        F_hi, F_lo = sb("F_hi", [P, C, B], F32R), sb("F_lo", [P, C, B], F32R)
        z = sb("z", [P, C, D])
        zT_hi, zT_lo = sb("zT_hi", [P, C, D], F32R), sb("zT_lo", [P, C, D], F32R)
        norm_bc = sb("norm_bc", [P, B])
        expo = sb("expo", [P, 2, B])
        F_raw = sb("F_raw", [P, 2, B])
        y = sb("y", [P, 2, D])
        late = sb("late", [P, 8, D])
        re2, im2, mag, y2 = late[:, 0:2], late[:, 2:4], late[:, 4:6], late[:, 6:8]
        o_tile = sb("o_tile", [P, 2, D])
        unused = sb("unused", [P, D])
        trig = sb("trig", [P, 8, D])
        ab = sb("ab", [P, C])
        neg_half_ab = sb("neg_half_ab", [P, C])
        AB = sb("AB", [P, C])
        W_scale = sb("W_scale", [P, C])
        norm_col = sb("norm_col", [P, C])
        stats = sb("stats", [P, C, 6])
        mv = sb("mv", [P, C, 2])
        var_eps = sb("var_eps", [P, C])
        rstd = sb("rstd", [P, C])
        stats2 = sb("stats2", [P, C, 6])
        mv2 = sb("mv2", [P, C, 2])
        var_eps2 = sb("var_eps2", [P, C])
        rstd2 = sb("rstd2", [P, C])
        neg_half = sb("neg_half", [P, 1])
        eps = sb("eps", [P, 1])
        ident = sb("ident", [P, P])

        project_ps = [bank(f"project_ps{k}") for k in range(2)]
        turn_ps = [bank(f"turn_ps{k}") for k in range(2)]
        token_ps = [bank(f"token_ps{k}") for k in range(4)]

        xis_loaded, gs_loaded, wT_loaded = sem("xis_loaded"), sem("gs_loaded"), sem("wT_loaded")
        theta_loaded, phi_loaded = sem("theta_loaded"), sem("phi_loaded")
        xT_loaded = sem("xT_loaded")
        x_loaded = [sem("x_loaded_even"), sem("x_loaded_odd")]
        norms_stored, norms_loaded = sem("norms_stored"), sem("norms_loaded")
        out_stored = [sem("out_stored_0"), sem("out_stored_1")]
        ident_made, exponent_set, half_ab_made = sem("ident_made"), sem("exponent_set"), sem("half_ab_made")
        gs_hi_made, gs_lo_made = sem("gs_hi_made"), sem("gs_lo_made")
        wT_hi_made, wT_lo_made = sem("wT_hi_made"), sem("wT_lo_made")
        AB_made, W_scale_made = sem("AB_made"), sem("W_scale_made")
        W_hi_made, W_made = sem("W_hi_made"), sem("W_made")
        trig_step, turns_made = sem("trig_step"), sem("turns_made")
        angle_step, angle_made = sem("angle_step"), sem("angle_made")
        sine_made, trig_made = sem("sine_made"), sem("trig_made")
        sumsq_done = sem("sumsq_done")
        xT_hi_made, xT_lo_made = sem("xT_hi_made"), sem("xT_lo_made")
        project_done, expo_made, exp_done, F_made = sem("project_done"), sem("expo_made"), sem("exp_done"), sem("F_made")
        mix_done, y_made, stats_made, mv_made = sem("mix_done"), sem("y_made"), sem("stats_made"), sem("mv_made")
        var_made, rstd_made, z_made = sem("var_made"), sem("rstd_made"), sem("z_made")
        turn_done, zT_hi_made, zT_made = sem("turn_done"), sem("zT_hi_made"), sem("zT_made")
        phase_done, square_done, sum_made, mag_made = sem("phase_done"), sem("square_done"), sem("sum_made"), sem("mag_made")
        y2_made, stats2_made, mv2_made = sem("y2_made"), sem("stats2_made"), sem("mv2_made")
        var2_made, rstd2_made, out_made = sem("var2_made"), sem("rstd2_made"), sem("out_made")

        TURN_CREDIT = 2
        SQUARE_CREDIT = 2 * C
        STORE_CREDIT = 16

        block = ctx.enter_context(nc.Block())


        @block.sync
        def _(sp):
            def turn_norms(q):
                if not isinstance(q, int) or q > 0:
                    sp.wait_ge(expo_made, C * q)
                sp.wait_ge(sumsq_done, C * (q + 1))
                sp.dma_start(norms_dram.rearrange("(c p) -> p c", p=P), norm_col[:, :],
                             allow_slow_non_contiguous=True).then_inc(norms_stored, 16)
                sp.wait_ge(norms_stored, 16 * (q + 1))
                sp.dma_start(norm_bc[:, :], norms_dram.partition_broadcast(P)).then_inc(norms_loaded, 16)

            def store_out(b, j):
                sp.wait_ge(out_made, C * b + j + 1)
                sp.dma_start(out_tiles[b][j], o_tile[:, j % 2, :]).then_inc(out_stored[j % 2], 16)

            sp.sem_inc(out_stored[0], STORE_CREDIT)
            sp.sem_inc(out_stored[1], STORE_CREDIT)
            sp.dma_start(trig[:, 0:C, :], by_chunk(gsT)).then_inc(gs_loaded, 16)
            sp.dma_start(xT_raw[:, :, :], xT_blocks[0]).then_inc(xT_loaded, 16)
            sp.dma_start(x_tok[:, 0], x_blocks[0]).then_inc(x_loaded[0], 16)
            turn_norms(0)
            sp.dma_start(x_tok[:, 1], x_blocks[1]).then_inc(x_loaded[1], 16)
            sp.dma_start(trig[:, C:2 * C, :], by_chunk(theta_noise)).then_inc(theta_loaded, 16)
            sp.wait_ge(gs_lo_made, C)
            sp.dma_start(trig[:, 0:C, :], by_chunk(theta)).then_inc(theta_loaded, 16)
            sp.dma_start(late[:, 0:C, :], by_chunk(phi)).then_inc(phi_loaded, 16)
            sp.dma_start(late[:, C:2 * C, :], by_chunk(phi_noise)).then_inc(phi_loaded, 16)
            sp.wait_ge(xT_lo_made, C)
            sp.dma_start(xT_raw[:, :, :], xT_blocks[1]).then_inc(xT_loaded, 16)
            turn_norms(1)
            turn_norms(2)

            def step(b, pair, slot, ahead):
                if ahead:
                    sp.wait_ge(xT_lo_made, C * (b + 2))
                    sp.dma_start(xT_raw[:, :, :], xT_blocks[b + 2]).then_inc(xT_loaded, 16)
                    sp.wait_ge(y_made, C * (b + 1))
                    sp.dma_start(x_tok[:, slot], x_blocks[b + 2]).then_inc(x_loaded[slot], 16)
                for j in range(C):
                    if ahead and j == 2:
                        turn_norms(b + 3)
                    store_out(b, j)

            with sp.Fori(0, NB // 2 - 1) as pair:
                for slot in range(2):
                    step(pair * 2 + slot, pair, slot, True)
            for slot in range(2):
                step(NB - 2 + slot, NB // 2 - 1, slot, False)
            for k in range(2):
                sp.wait_ge(out_stored[k], STORE_CREDIT + 16 * NB * C // 2)

        @block.gpsimd
        def _(pool):
            pool.memset(neg_half[:, :], -0.5).then_inc(exponent_set, 1)
            pool.memset(eps[:, :], EPS).then_inc(exponent_set, 1)
            pool.memset(ident[:, :], 0.0).then_inc(ident_made, 1)
            pool.wait_ge(ident_made, 1)
            pool.affine_select(out=ident[:, :], in_=ident[:, :], compare_op=ALU.not_equal, fill=1.0,
                               base=0, pattern=[[-1, P]], channel_multiplier=1).then_inc(ident_made, 1)

            steps = 0
            for buf, loaded, shift in ((trig, theta_loaded, HALF_PI), (late, phi_loaded, 0.0)):
                pool.wait_ge(loaded, 32)
                for c in range(C):
                    angle, turns = buf[:, c, :], buf[:, C + c, :]
                    pool.tensor_tensor(angle, angle, turns, ALU.add).then_inc(trig_step, 1)
                    pool.wait_ge(trig_step, steps + 1)
                    pool.tensor_scalar(turns, angle, shift, 1.0 / (2 * np.pi), ALU.add, ALU.mult).then_inc(trig_step, 1)
                    pool.wait_ge(trig_step, steps + 2)
                    pool.tensor_scalar(turns, turns, ROUNDER, -ROUNDER, ALU.add, ALU.add).then_inc(turns_made, 1)
                    steps += 2

            def inverse_root(b, j, mv_ready, moments, shifted, shifted_made, root, root_made):
                n = C * b + j + 1
                pool.wait_ge(mv_ready, n)
                pool.tensor_tensor(shifted[:, j:j + 1], moments[:, j, 1:2], eps[:, :], ALU.add).then_inc(shifted_made, 1)
                pool.wait_ge(shifted_made, n)
                pool.tensor_tensor(root[:, j:j + 1], shifted[:, j:j + 1], neg_half[:, :], ALU.pow).then_inc(root_made, 1)

            def step(b):
                for j in range(C):
                    inverse_root(b, j, mv_made, mv, var_eps, var_made, rstd, rstd_made)
                for j in range(C):
                    inverse_root(b, j, mv2_made, mv2, var_eps2, var2_made, rstd2, rstd2_made)

            pool.wait_ge(exponent_set, 2)
            with pool.Fori(0, NB) as b:
                step(b)

        @block.scalar
        def _(act):
            act.sem_inc(square_done, SQUARE_CREDIT)
            act.dma_start(z[:, :, :], by_chunk(wT)).then_inc(wT_loaded, 16)
            act.dma_start(x_tok[:, 1], by_chunk(w)).then_inc(x_loaded[1], 16)
            act.dma_start(ab[:, :], xis.rearrange("(c p) -> p c", p=P),
                          allow_slow_non_contiguous=True).then_inc(xis_loaded, 16)

            def sum_square(q, j, slot):
                if not (isinstance(q, int) and C * q + j == 0):
                    act.wait_ge(sumsq_done, C * q + j)
                nc.scalar.activation(unused[:, :], x_tok[:, slot, j, :], ACT.Square,
                                     accum_out=norm_col[:, j:j + 1]).then_inc(sumsq_done, 1)

            def sum_squares(q, slot):
                for j in range(C):
                    sum_square(q, j, slot)

            def split_hi(b):
                act.wait_ge(xT_loaded, 16 * (b + 1))
                for c in range(C):
                    nc.scalar.activation(xT_hi[:, c, :], xT_raw[:, c, :], ACT.Copy).then_inc(xT_hi_made, 1)

            act.wait_ge(gs_loaded, 16)
            for c in range(C):
                nc.scalar.activation(gs_hi[:, c, :], trig[:, c, :], ACT.Copy).then_inc(gs_hi_made, 1)
            act.wait_ge(wT_loaded, 16)
            for c in range(C):
                nc.scalar.activation(zT_hi[:, c, :], z[:, c, :], ACT.Copy).then_inc(wT_hi_made, 1)
            act.wait_ge(x_loaded[1], 16)
            sum_squares(0, 1)
            split_hi(0)
            act.wait_ge(xis_loaded, 16)
            nc.scalar.activation(AB[:, :], ab[:, :], ACT.Exp).then_inc(AB_made, 1)
            act.wait_ge(x_loaded[0], 16)
            act.wait_ge(norms_stored, 16)
            sum_squares(1, 0)
            for j in range(C):
                act.wait_ge(expo_made, j + 1)
                nc.scalar.activation(F_raw[:, j % 2, :], expo[:, j % 2, :], ACT.Exp,
                                     scale=ab[:, j:j + 1]).then_inc(exp_done, 2)

            def features(q, j):
                act.wait_ge(expo_made, C * q + j + 1)
                nc.scalar.activation(F_hi[:, j, :], expo[:, j % 2, :], ACT.Exp,
                                     scale=ab[:, j:j + 1]).then_inc(exp_done, 1)
                nc.scalar.activation(F_raw[:, j % 2, :], expo[:, j % 2, :], ACT.Exp,
                                     scale=ab[:, j:j + 1]).then_inc(exp_done, 1)

            for j in range(C):
                features(1, j)
            act.wait_ge(project_done, 2 * C)
            split_hi(1)
            act.wait_ge(x_loaded[1], 32)
            act.wait_ge(norms_stored, 32)
            sum_squares(2, 1)

            n = 0
            for buf, hi in ((trig, cos_hi), (late, sin_hi)):
                for c in range(C):
                    n += 1
                    act.wait_ge(angle_made, n)
                    nc.scalar.activation(hi[:, c, :], buf[:, c, :], ACT.Sin).then_inc(sine_made, 1)
                    nc.scalar.activation(buf[:, C + c, :], buf[:, c, :], ACT.Sin).then_inc(sine_made, 1)

            def step(b, pair, slot, more, ahead):
                for j in range(C):
                    act.wait_ge(turn_done, C * b + j + 1)
                    nc.scalar.activation(zT_hi[:, j, :], turn_ps[j % 2][:, :], ACT.Copy).then_inc(zT_hi_made, 1)
                    if more:
                        features(b + 2, j)

                def magnitude(j):
                    act.wait_ge(sum_made, C * b + j + 1)
                    nc.scalar.activation(mag[:, j % 2, :], re2[:, j % 2, :], ACT.Sqrt).then_inc(mag_made, 1)

                if ahead:
                    act.wait_ge(xT_loaded, 16 * (b + 3))
                    act.wait_ge(x_loaded[slot], 16 * (pair + 2 + slot))
                for j in range(C):
                    if j >= 2:
                        act.wait_ge(mag_made, C * b + j - 1)
                    for part, dst in ((0, re2), (1, im2)):
                        act.wait_ge(phase_done, 2 * C * b + 2 * j + part + 1)
                        nc.scalar.activation(dst[:, j % 2, :], token_ps[(2 * j + part) % 4][:, :],
                                             ACT.Square).then_inc(square_done, 1)
                        if part == 0 and j >= 1:
                            magnitude(j - 1)
                    if ahead:
                        nc.scalar.activation(xT_hi[:, j, :], xT_raw[:, j, :], ACT.Copy).then_inc(xT_hi_made, 1)
                        sum_square(b + 3, j, slot)
                magnitude(C - 1)

            with act.Fori(0, NB // 2 - 1) as pair:
                for slot in range(2):
                    step(pair * 2 + slot, pair, slot, True, True)
            step(NB - 2, NB // 2 - 1, 0, True, False)
            step(NB - 1, NB // 2 - 1, 1, False, False)

        @block.tensor
        def _(pe):
            def project(q, j, rhs_hi, rhs_lo):
                if not (isinstance(q, int) and q == 0 and j < 2):
                    pe.wait_ge(expo_made, C * q + j - 1)
                o = project_ps[j % 2][:, :]
                cols = slice(j * P, (j + 1) * P)
                for c in range(C):
                    nc.tensor.matmul(o, gs_hi[:, c, cols], rhs_hi[:, c, :], start=(c == 0), stop=False)
                    nc.tensor.matmul(o, gs_hi[:, c, cols], rhs_lo[:, c, :], start=False, stop=False)
                    last = nc.tensor.matmul(o, gs_lo[:, c, cols], rhs_hi[:, c, :], start=False, stop=(c == C - 1))
                last.then_inc(project_done, 1)

            def product(o, left_hi, left_lo, right_hi, right_lo):
                for c in range(C):
                    nc.tensor.matmul(o, left_hi[c], right_hi[:, c, :], start=(c == 0), stop=False)
                    nc.tensor.matmul(o, left_hi[c], right_lo[:, c, :], start=False, stop=False)
                    last = nc.tensor.matmul(o, left_lo[c], right_hi[:, c, :], start=False, stop=(c == C - 1))
                return last

            pe.wait_ge(gs_lo_made, C)
            pe.wait_ge(wT_lo_made, C)
            for j in range(C):
                project(0, j, zT_hi, zT_lo)
            pe.wait_ge(xT_lo_made, C)
            for j in range(C):
                project(1, j, xT_hi, xT_lo)
            pe.wait_ge(ident_made, 2)
            pe.wait_ge(W_made, C)

            def step(b, more, first_phase=False):
                pe.wait_ge(F_made, C * (b + 1))
                for j in range(C):
                    pe.wait_ge(square_done, 2 * C * b + SQUARE_CREDIT - C + j + 1)
                    cols = slice(j * P, (j + 1) * P)
                    product(token_ps[j][:, :], [F_hi[:, c, cols] for c in range(C)], [F_lo[:, c, cols] for c in range(C)],
                            W_hi, W_lo).then_inc(mix_done, 1)
                if more:
                    pe.wait_ge(xT_lo_made, C * (b + 2))
                for j in range(C):
                    if more:
                        project(b + 2, j, xT_hi, xT_lo)
                    pe.wait_ge(z_made, C * b + j + 1)
                    pe.wait_ge(zT_made, C * b + j - 1 + TURN_CREDIT)
                    for c in range(C):
                        last = nc.tensor.transpose(turn_ps[j % 2][:, c * P:(c + 1) * P], z[:, j, c * P:(c + 1) * P], ident[:, :])
                    last.then_inc(turn_done, 1)
                if first_phase:
                    pe.wait_ge(trig_made, 2 * C)
                for j in range(C):
                    pe.wait_ge(zT_made, C * b + j + 1 + TURN_CREDIT)
                    for part, (hi, lo) in enumerate(((cos_hi, cos_lo), (sin_hi, sin_lo))):
                        use = 2 * j + part
                        if use < 4:
                            pe.wait_ge(y_made, C * b + use + 1)
                        else:
                            pe.wait_ge(square_done, 2 * C * b + SQUARE_CREDIT + use - 3)
                        cols = [slice(c * P, (c + 1) * P) for c in range(C)]
                        product(token_ps[use % 4][:, :], [zT_hi[:, j, s] for s in cols], [zT_lo[:, j, s] for s in cols],
                                hi, lo).then_inc(phase_done, 1)

            step(0, True, True)
            with pe.Fori(1, NB - 1) as b:
                step(b, True)
            step(NB - 1, False)

        @block.vector
        def _(dve):
            dve.sem_inc(zT_made, TURN_CREDIT)
            tt, ts, stt = nc.vector.tensor_tensor, nc.vector.tensor_scalar, nc.vector.scalar_tensor_tensor

            def lower(dst, whole, hi):
                return tt(dst, whole, hi.bitcast(F32), ALU.subtract)

            def exponent(q, j):
                dve.wait_ge(project_done, C * q + j + 1)
                stt(out=expo[:, j % 2, :], in0=norm_bc[:, :], scalar=neg_half_ab[:, j:j + 1],
                    in1=project_ps[j % 2][:, :], op0=ALU.mult, op1=ALU.add).then_inc(expo_made, 1)

            def split_features(q, j):
                dve.wait_ge(exp_done, 2 * (C * q + j + 1))
                lower(F_lo[:, j, :], F_raw[:, j % 2, :], F_hi[:, j, :]).then_inc(F_made, 1)

            def split_lo(b, c):
                dve.wait_ge(xT_hi_made, C * b + c + 1)
                lower(xT_lo[:, c, :], xT_raw[:, c, :], xT_hi[:, c, :]).then_inc(xT_lo_made, 1)

            for c in range(C):
                dve.wait_ge(gs_hi_made, c + 1)
                lower(gs_lo[:, c, :], trig[:, c, :], gs_hi[:, c, :]).then_inc(gs_lo_made, 1)
            for c in range(C):
                dve.wait_ge(wT_hi_made, c + 1)
                lower(zT_lo[:, c, :], z[:, c, :], zT_hi[:, c, :]).then_inc(wT_lo_made, 1)
            dve.wait_ge(xis_loaded, 16)
            ts(neg_half_ab[:, :], ab[:, :], -0.5, None, ALU.mult).then_inc(half_ab_made, 1)
            for c in range(C):
                split_lo(0, c)
            dve.wait_ge(AB_made, 1)
            stt(out=W_scale[:, :], in0=AB[:, :], scalar=1.0 / R, in1=AB[:, :],
                op0=ALU.mult, op1=ALU.mult).then_inc(W_scale_made, 1)
            dve.wait_ge(half_ab_made, 1)
            dve.wait_ge(W_scale_made, 1)
            dve.wait_ge(norms_loaded, 16)
            for j in range(C):
                exponent(0, j)
                dve.wait_ge(exp_done, 2 * (j + 1))
                ts(W_hi[:, j, :], F_raw[:, j % 2, :], W_scale[:, j:j + 1], None, ALU.mult).then_inc(W_hi_made, 1)
                dve.wait_ge(W_hi_made, j + 1)
                stt(out=W_lo[:, j, :], in0=F_raw[:, j % 2, :], scalar=W_scale[:, j:j + 1],
                    in1=W_hi[:, j, :].bitcast(F32), op0=ALU.mult, op1=ALU.subtract).then_inc(W_made, 1)

            steps = 0
            def reduce_angle(buf, c, shift, n):
                nonlocal steps
                angle, turns = buf[:, c, :], buf[:, C + c, :]
                dve.wait_ge(turns_made, n)
                for part in (TWO_PI_A, TWO_PI_B, TWO_PI_C):
                    stt(out=angle, in0=turns, scalar=-part, in1=angle, op0=ALU.mult, op1=ALU.add).then_inc(angle_step, 1)
                    steps += 1
                    dve.wait_ge(angle_step, steps)
                ts(angle, angle, shift, PI_INSIDE, ALU.add, ALU.min).then_inc(angle_step, 1)
                steps += 1
                dve.wait_ge(angle_step, steps)
                ts(angle, angle, -PI_INSIDE, None, ALU.max).then_inc(angle_made, 1)

            dve.wait_ge(norms_loaded, 32)
            for j in range(C):
                exponent(1, j)
                reduce_angle(trig, j, HALF_PI, j + 1)
                split_features(1, j)
            for c in range(C):
                split_lo(1, c)
                reduce_angle(late, c, 0.0, C + c + 1)
            n = 0
            for buf, hi, lo in ((trig, cos_hi, cos_lo), (late, sin_hi, sin_lo)):
                for c in range(C):
                    n += 2
                    dve.wait_ge(sine_made, n)
                    lower(lo[:, c, :], buf[:, C + c, :], hi[:, c, :]).then_inc(trig_made, 1)

            def halves(n, j, src, src_made, st, st_made):
                dve.wait_ge(src_made, n)
                nc.vector.bn_stats(st[:, j, :], src).then_inc(st_made, 1)

            def moments(j, st, m, m_made):
                nc.vector.bn_aggr(m[:, j, :], st[:, j, :]).then_inc(m_made, 1)

            def normalise(n, j, dst, src, root_made, m, root, dst_made):
                dve.wait_ge(root_made, n)
                ts(dst, src, m[:, j, 0:1], root[:, j:j + 1], ALU.subtract, ALU.mult).then_inc(dst_made, 1)

            def step(b, pair, slot, more, ahead):
                n = [C * b + j + 1 for j in range(C)]
                dve.wait_ge(x_loaded[slot], 16 * (pair + 1 + slot))

                def residual1(j):
                    if j >= 2:
                        dve.wait_ge(z_made, n[j - 2])
                    dve.wait_ge(mix_done, n[j])
                    tt(y[:, j % 2, :], token_ps[j][:, :], x_tok[:, slot, j, :], ALU.add).then_inc(y_made, 1)

                def norm1(j):
                    normalise(n[j], j, z[:, j, :], y[:, j % 2, :], rstd_made, mv, rstd, z_made)

                for j in range(C):
                    if j == 1:
                        dve.wait_ge(stats_made, n[0])
                    residual1(j)
                    if j == 1:
                        moments(0, stats, mv, mv_made)
                    halves(n[j], j, y[:, j % 2, :], y_made, stats, stats_made)
                    if j >= 1:
                        dve.wait_ge(stats_made, n[j])
                        norm1(j - 1)
                        moments(j, stats, mv, mv_made)
                norm1(C - 1)

                if more:
                    dve.wait_ge(norms_loaded, 16 * (b + 3))
                for j in range(C):
                    if more:
                        exponent(b + 2, j)
                    dve.wait_ge(zT_hi_made, n[j])
                    lower(zT_lo[:, j, :], turn_ps[j % 2][:, :], zT_hi[:, j, :]).then_inc(zT_made, 1)
                    if more:
                        split_features(b + 2, j)

                def residual2(j):
                    if j >= 2:
                        dve.wait_ge(out_made, n[j - 2])
                    dve.wait_ge(mag_made, n[j])
                    tt(y2[:, j % 2, :], z[:, j, :], mag[:, j % 2, :], ALU.add).then_inc(y2_made, 1)
                    halves(n[j], j, y2[:, j % 2, :], y2_made, stats2, stats2_made)
                    dve.wait_ge(stats2_made, n[j])

                def norm2(j):
                    dve.wait_ge(out_stored[j % 2], 32 * b + 16 * (j // 2) + STORE_CREDIT)
                    normalise(n[j], j, o_tile[:, j % 2, :], y2[:, j % 2, :], rstd2_made, mv2, rstd2, out_made)

                for j in range(C):
                    if j >= 1:
                        residual2(j - 1)
                    if ahead:
                        split_lo(b + 2, j)
                    if j >= 1:
                        moments(j - 1, stats2, mv2, mv2_made)
                    if j >= 2:
                        norm2(j - 2)
                    dve.wait_ge(square_done, 2 * C * b + 2 * j + 2 + SQUARE_CREDIT)
                    tt(re2[:, j % 2, :], re2[:, j % 2, :], im2[:, j % 2, :], ALU.add).then_inc(sum_made, 1)
                residual2(C - 1)
                norm2(C - 2)
                moments(C - 1, stats2, mv2, mv2_made)
                norm2(C - 1)

            with dve.Fori(0, NB // 2 - 1) as pair:
                for slot in range(2):
                    step(pair * 2 + slot, pair, slot, True, True)
            step(NB - 2, NB // 2 - 1, 0, True, False)
            step(NB - 1, NB // 2 - 1, 1, False, False)


def kernel(**inputs):
    import concourse.bacc as _bacc
    from concourse.bass_utils import run_bass_kernel_spmd as _run

    x = np.asarray(inputs["L0_attn_x"])
    tokens = x.reshape(-1, x.shape[-1])
    w = np.asarray(inputs["L0_attn_input_weights"])
    gs = np.asarray(inputs["L0_attn_proj_matrix"])
    laid = {
        "xT": tokens.T, "x": tokens, "wT": w.T, "w": w, "xis": inputs["L0_attn_xis"], "gsT": gs.T,
        "theta": inputs["L0_ffn_theta"], "phi": inputs["L0_ffn_phi"],
        "theta_noise": inputs["L0_ffn_theta_noise"], "phi_noise": inputs["L0_ffn_phi_noise"],
    }
    nc = _bacc.Bacc("TRN2", target_bir_lowering=False, num_devices=1)
    arrays, args = {}, []
    for name, a in laid.items():
        a = np.ascontiguousarray(a)
        arrays[f"in_{name}"] = a
        args.append(nc.dram_tensor(f"in_{name}", a.shape, mybir.dt.from_np(a.dtype), kind="ExternalInput").ap())
    args.append(nc.dram_tensor("out_tokens", tokens.shape, F32, kind="ExternalOutput").ap())
    build(nc, *args)
    r = _run(nc, [arrays], core_ids=[0])
    return r.results[0]["out_tokens"].reshape(x.shape)
```

```python
from contextlib import ExitStack

import numpy as np

import concourse.bass as bass
from concourse import mybir

P = 128
ALU = mybir.AluOpType
ACT = mybir.ActivationFunctionType
F32 = mybir.dt.float32
F32R = mybir.dt.float32r

EPS = 1e-5
TWO_PI_A = 6.28125
TWO_PI_B = float(np.float32(2 * np.pi - TWO_PI_A))
ROUNDER = 1.5 * 2.0**23
PI_INSIDE = float(np.nextafter(np.float32(np.pi), np.float32(0)))
HALF_PI = float(np.float32(np.pi / 2))


def build(nc, xT, x, wT, w, xis, gsT, theta, phi, theta_noise, phi_noise, out):
    T, D = x.shape
    R = gsT.shape[1]
    O = w.shape[0]
    B = 512
    NB = T // B
    C = D // P
    assert D == R == O == B == C * P and T % (2 * B) == 0 and NB >= 4

    xT_blocks = xT.rearrange("(c p) (b t) -> b p c t", p=P, t=B)
    x_blocks = x.rearrange("(b c p) d -> b p c d", p=P, c=C)
    out_tiles = out.rearrange("(b c p) d -> b c p d", p=P, c=C)
    by_chunk = lambda m: m.rearrange("(c p) n -> p c n", p=P)
    norms_dram = [nc.dram_tensor(f"token_norms_{k}", (B,), F32, kind="Internal").ap() for k in range(2)]

    with ExitStack() as ctx:
        sb = lambda name, shape, dt=F32: ctx.enter_context(nc.sbuf_tensor(name, shape, dt))
        bank = lambda name: ctx.enter_context(nc.psum_tensor(name, [P, 512], F32))
        sem = lambda name: ctx.enter_context(nc.semaphore(name))

        gs_hi, gs_lo = sb("gs_hi", [P, C, R], F32R), sb("gs_lo", [P, C, R], F32R)
        W_hi, W_lo = sb("W_hi", [P, C, O], F32R), sb("W_lo", [P, C, O], F32R)
        cos_hi, cos_lo = sb("cos_hi", [P, C, O], F32R), sb("cos_lo", [P, C, O], F32R)
        sin_hi, sin_lo = sb("sin_hi", [P, C, O], F32R), sb("sin_lo", [P, C, O], F32R)
        xT_raw = sb("xT_raw", [P, C, B])
        xT_hi, xT_lo = sb("xT_hi", [P, C, B], F32R), sb("xT_lo", [P, C, B], F32R)
        x_tok = sb("x_tok", [P, 2, C, D])
        F_hi, F_lo = sb("F_hi", [P, C, B], F32R), sb("F_lo", [P, C, B], F32R)
        z = sb("z", [P, C, D])
        zT_hi, zT_lo = sb("zT_hi", [P, C, D], F32R), sb("zT_lo", [P, C, D], F32R)
        norm_bc = sb("norm_bc", [P, 2, B])
        expo = sb("expo", [P, 2, B])
        F_raw = sb("F_raw", [P, 2, B])
        y = sb("y", [P, 2, D])
        late = sb("late", [P, 8, D])
        re2, im2, mag, y2 = late[:, 0:2], late[:, 2:4], late[:, 4:6], late[:, 6:8]
        o_tile = sb("o_tile", [P, 2, D])
        unused = sb("unused", [P, D])
        trig = sb("trig", [P, 8, D])
        ab = sb("ab", [P, C])
        neg_half_ab = sb("neg_half_ab", [P, C])
        AB = sb("AB", [P, C])
        W_scale = sb("W_scale", [P, C])
        norm_col = sb("norm_col", [P, 2, C])
        stats = sb("stats", [P, C, 6])
        mv = sb("mv", [P, C, 2])
        var_eps = sb("var_eps", [P, C])
        rstd = sb("rstd", [P, C])
        stats2 = sb("stats2", [P, C, 6])
        mv2 = sb("mv2", [P, C, 2])
        var_eps2 = sb("var_eps2", [P, C])
        rstd2 = sb("rstd2", [P, C])
        neg_half = sb("neg_half", [P, 1])
        eps = sb("eps", [P, 1])
        ident = sb("ident", [P, P])

        project_ps = [bank(f"project_ps{k}") for k in range(2)]
        turn_ps = [bank(f"turn_ps{k}") for k in range(2)]
        token_ps = [bank(f"token_ps{k}") for k in range(4)]

        xis_loaded = sem("xis_loaded")
        gs_loaded = [sem(f"gs_loaded_{c}") for c in range(C)]
        wT_loaded = [sem(f"wT_loaded_{c}") for c in range(C)]
        theta_loaded, phi_loaded = sem("theta_loaded"), sem("phi_loaded")
        xT_loaded = sem("xT_loaded")
        x_loaded = [sem("x_loaded_even"), sem("x_loaded_odd")]
        norms_stored, norms_loaded = sem("norms_stored"), sem("norms_loaded")
        out_stored = [sem("out_stored_0"), sem("out_stored_1")]
        ident_made, exponent_set, half_ab_made = sem("ident_made"), sem("exponent_set"), sem("half_ab_made")
        gs_hi_made, gs_lo_made = sem("gs_hi_made"), sem("gs_lo_made")
        wT_hi_made, wT_lo_made = sem("wT_hi_made"), sem("wT_lo_made")
        AB_made, W_scale_made = sem("AB_made"), sem("W_scale_made")
        W_hi_made, W_made = sem("W_hi_made"), sem("W_made")
        trig_step, turns_made = sem("trig_step"), sem("turns_made")
        angle_step, angle_made = sem("angle_step"), sem("angle_made")
        sine_made, trig_made = sem("sine_made"), sem("trig_made")
        sumsq_done = sem("sumsq_done")
        xT_hi_made, xT_lo_made = sem("xT_hi_made"), sem("xT_lo_made")
        project_done, expo_made, exp_done, F_made = sem("project_done"), sem("expo_made"), sem("exp_done"), sem("F_made")
        mix_done, y_made, stats_made, mv_made = sem("mix_done"), sem("y_made"), sem("stats_made"), sem("mv_made")
        var_made, rstd_made, z_made = sem("var_made"), sem("rstd_made"), sem("z_made")
        turn_done, zT_hi_made, zT_made = sem("turn_done"), sem("zT_hi_made"), sem("zT_made")
        phase_done, square_done, sum_made, mag_made = sem("phase_done"), sem("square_done"), sem("sum_made"), sem("mag_made")
        y2_made, stats2_made, mv2_made = sem("y2_made"), sem("stats2_made"), sem("mv2_made")
        var2_made, rstd2_made, out_made = sem("var2_made"), sem("rstd2_made"), sem("out_made")

        TURN_CREDIT = 2
        SQUARE_CREDIT = 2 * C
        STORE_CREDIT = 16

        block = ctx.enter_context(nc.Block())


        @block.sync
        def _(sp):
            def turn_norms(q, k):
                sp.wait_ge(sumsq_done, C * (q + 1))
                sp.dma_start(norms_dram[k].rearrange("(c p) -> p c", p=P), norm_col[:, k, :],
                             allow_slow_non_contiguous=True).then_inc(norms_stored, 16)
                sp.wait_ge(norms_stored, 16 * (q + 1))
                sp.dma_start(norm_bc[:, k, :], norms_dram[k].partition_broadcast(P)).then_inc(norms_loaded, 16)

            def store_out(b, j):
                sp.wait_ge(out_made, C * b + j + 1)
                sp.dma_start(out_tiles[b][j], o_tile[:, j % 2, :]).then_inc(out_stored[j % 2], 16)

            sp.sem_inc(out_stored[0], STORE_CREDIT)
            sp.sem_inc(out_stored[1], STORE_CREDIT)
            for c in range(C):
                sp.dma_start(trig[:, c, :], by_chunk(gsT)[:, c, :]).then_inc(gs_loaded[c], 16)
            sp.dma_start(xT_raw[:, :, :], xT_blocks[0]).then_inc(xT_loaded, 16)
            sp.dma_start(x_tok[:, 0], x_blocks[0]).then_inc(x_loaded[0], 16)
            sp.dma_start(trig[:, C:2 * C, :], by_chunk(theta_noise)).then_inc(theta_loaded, 16)
            sp.wait_ge(gs_lo_made, C)
            sp.dma_start(trig[:, 0:C, :], by_chunk(theta)).then_inc(theta_loaded, 16)
            turn_norms(0, 0)
            sp.wait_ge(xT_lo_made, C)
            sp.dma_start(xT_raw[:, :, :], xT_blocks[1]).then_inc(xT_loaded, 16)
            sp.wait_ge(norms_loaded, 16)
            turn_norms(1, 1)
            sp.dma_start(late[:, 0:C, :], by_chunk(phi)).then_inc(phi_loaded, 16)
            sp.dma_start(late[:, C:2 * C, :], by_chunk(phi_noise)).then_inc(phi_loaded, 16)
            sp.dma_start(x_tok[:, 1], x_blocks[1]).then_inc(x_loaded[1], 16)
            sp.wait_ge(norms_loaded, 32)
            sp.wait_ge(expo_made, C)
            turn_norms(2, 0)

            def step(b, pair, slot, ahead):
                if ahead:
                    sp.wait_ge(xT_lo_made, C * (b + 2))
                    sp.dma_start(xT_raw[:, :, :], xT_blocks[b + 2]).then_inc(xT_loaded, 16)
                    sp.wait_ge(y_made, C * (b + 1))
                    sp.dma_start(x_tok[:, slot], x_blocks[b + 2]).then_inc(x_loaded[slot], 16)
                for j in range(C):
                    if ahead and j == 2:
                        sp.wait_ge(expo_made, C * (b + 3))
                        turn_norms(b + 3, 1 - slot)
                    store_out(b, j)

            with sp.Fori(0, NB // 2 - 1) as pair:
                for slot in range(2):
                    step(pair * 2 + slot, pair, slot, True)
            for slot in range(2):
                step(NB - 2 + slot, NB // 2 - 1, slot, False)
            for k in range(2):
                sp.wait_ge(out_stored[k], STORE_CREDIT + 16 * NB * C // 2)

        @block.gpsimd
        def _(pool):
            pool.memset(neg_half[:, :], -0.5).then_inc(exponent_set, 1)
            pool.memset(eps[:, :], EPS).then_inc(exponent_set, 1)
            pool.memset(ident[:, :], 0.0).then_inc(ident_made, 1)
            pool.wait_ge(ident_made, 1)
            pool.affine_select(out=ident[:, :], in_=ident[:, :], compare_op=ALU.not_equal, fill=1.0,
                               base=0, pattern=[[-1, P]], channel_multiplier=1).then_inc(ident_made, 1)

            def less(dst, whole, hi, made):
                pool.tensor_tensor(dst, whole, hi.bitcast(F32), ALU.subtract).then_inc(made, 1)

            for c in range(C):
                pool.wait_ge(xT_hi_made, c + 1)
                less(xT_lo[:, c, :], xT_raw[:, c, :], xT_hi[:, c, :], xT_lo_made)

            steps = 0
            for buf, loaded, shift in ((trig, theta_loaded, HALF_PI), (late, phi_loaded, 0.0)):
                pool.wait_ge(loaded, 32)
                for c in range(C):
                    angle, turns = buf[:, c, :], buf[:, C + c, :]
                    pool.tensor_tensor(angle, angle, turns, ALU.add).then_inc(trig_step, 1)
                    steps += 1
                    pool.wait_ge(trig_step, steps)
                    if shift:
                        pool.tensor_scalar(angle, angle, shift, 1.0, ALU.add, ALU.mult).then_inc(trig_step, 1)
                        steps += 1
                        pool.wait_ge(trig_step, steps)
                    pool.tensor_scalar(turns, angle, 1.0 / (2 * np.pi), ROUNDER, ALU.mult, ALU.add).then_inc(trig_step, 1)
                    steps += 1
                    pool.wait_ge(trig_step, steps)
                    pool.tensor_scalar(turns, turns, -ROUNDER, 1.0, ALU.add, ALU.mult).then_inc(turns_made, 1)

            def inverse_root(b, j, mv_ready, moments, shifted, shifted_made, root, root_made):
                n = C * b + j + 1
                pool.wait_ge(mv_ready, n)
                pool.tensor_tensor(shifted[:, j:j + 1], moments[:, j, 1:2], eps[:, :], ALU.add).then_inc(shifted_made, 1)
                pool.wait_ge(shifted_made, n)
                pool.tensor_tensor(root[:, j:j + 1], shifted[:, j:j + 1], neg_half[:, :], ALU.pow).then_inc(root_made, 1)

            def step(b):
                for j in range(C):
                    inverse_root(b, j, mv_made, mv, var_eps, var_made, rstd, rstd_made)
                for j in range(C):
                    inverse_root(b, j, mv2_made, mv2, var_eps2, var2_made, rstd2, rstd2_made)

            pool.wait_ge(exponent_set, 2)
            with pool.Fori(0, NB) as b:
                step(b)

        @block.scalar
        def _(act):
            act.sem_inc(square_done, SQUARE_CREDIT)
            for c in range(C):
                act.dma_start(z[:, c, :], by_chunk(wT)[:, c, :]).then_inc(wT_loaded[c], 16)
            act.dma_start(x_tok[:, 1], by_chunk(w)).then_inc(x_loaded[1], 16)
            act.dma_start(ab[:, :], xis.rearrange("(c p) -> p c", p=P),
                          allow_slow_non_contiguous=True).then_inc(xis_loaded, 16)

            def sum_square(q, j, slot, k):
                if not (isinstance(q, int) and C * q + j == 0):
                    act.wait_ge(sumsq_done, C * q + j)
                nc.scalar.activation(unused[:, :], x_tok[:, slot, j, :], ACT.Square,
                                     accum_out=norm_col[:, k, j:j + 1]).then_inc(sumsq_done, 1)

            def sum_squares(q, slot):
                for j in range(C):
                    sum_square(q, j, slot, q % 2)

            def split_hi(b):
                act.wait_ge(xT_loaded, 16 * (b + 1))
                for c in range(C):
                    nc.scalar.activation(xT_hi[:, c, :], xT_raw[:, c, :], ACT.Copy).then_inc(xT_hi_made, 1)

            for c in range(C):
                act.wait_ge(gs_loaded[c], 16)
                nc.scalar.activation(gs_hi[:, c, :], trig[:, c, :], ACT.Copy).then_inc(gs_hi_made, 1)
                act.wait_ge(wT_loaded[c], 16)
                nc.scalar.activation(zT_hi[:, c, :], z[:, c, :], ACT.Copy).then_inc(wT_hi_made, 1)
            act.wait_ge(x_loaded[1], 16)
            sum_squares(0, 1)
            split_hi(0)
            act.wait_ge(xis_loaded, 16)
            nc.scalar.activation(AB[:, :], ab[:, :], ACT.Exp).then_inc(AB_made, 1)
            act.wait_ge(x_loaded[0], 16)
            sum_squares(1, 0)
            for j in range(C):
                act.wait_ge(expo_made, j + 1)
                if j >= 2:
                    act.wait_ge(W_made, j - 1)
                nc.scalar.activation(F_raw[:, j % 2, :], expo[:, j % 2, :], ACT.Exp,
                                     scale=ab[:, j:j + 1]).then_inc(exp_done, 2)

            def features(q, j):
                act.wait_ge(expo_made, C * q + j + 1)
                nc.scalar.activation(F_hi[:, j, :], expo[:, j % 2, :], ACT.Exp,
                                     scale=ab[:, j:j + 1]).then_inc(exp_done, 1)
                nc.scalar.activation(F_raw[:, j % 2, :], expo[:, j % 2, :], ACT.Exp,
                                     scale=ab[:, j:j + 1]).then_inc(exp_done, 1)

            for j in range(C):
                features(1, j)
            act.wait_ge(project_done, 2 * C)
            split_hi(1)
            act.wait_ge(x_loaded[1], 32)
            sum_squares(2, 1)

            def sines(buf, hi, n):
                for c in range(C):
                    act.wait_ge(angle_made, n + c + 1)
                    nc.scalar.activation(hi[:, c, :], buf[:, c, :], ACT.Sin).then_inc(sine_made, 1)
                    nc.scalar.activation(buf[:, C + c, :], buf[:, c, :], ACT.Sin).then_inc(sine_made, 1)

            sines(trig, cos_hi, 0)

            def step(b, pair, slot, more, ahead, first=False):
                for j in range(C):
                    act.wait_ge(turn_done, C * b + j + 1)
                    nc.scalar.activation(zT_hi[:, j, :], turn_ps[j % 2][:, :], ACT.Copy).then_inc(zT_hi_made, 1)
                    if more:
                        features(b + 2, j)

                def magnitude(j):
                    act.wait_ge(sum_made, C * b + j + 1)
                    nc.scalar.activation(mag[:, j % 2, :], re2[:, j % 2, :], ACT.Sqrt).then_inc(mag_made, 1)

                if first:
                    sines(late, sin_hi, C)
                    act.wait_ge(sine_made, 4 * C)
                if ahead:
                    act.wait_ge(xT_loaded, 16 * (b + 3))
                    act.wait_ge(x_loaded[slot], 16 * (pair + 2 + slot))
                for j in range(C):
                    if j >= 2:
                        act.wait_ge(mag_made, C * b + j - 1)
                    for part, dst in ((0, re2), (1, im2)):
                        act.wait_ge(phase_done, 2 * C * b + 2 * j + part + 1)
                        nc.scalar.activation(dst[:, j % 2, :], token_ps[(2 * j + part) % 4][:, :],
                                             ACT.Square).then_inc(square_done, 1)
                        if part == 0 and j >= 1:
                            magnitude(j - 1)
                    if ahead:
                        nc.scalar.activation(xT_hi[:, j, :], xT_raw[:, j, :], ACT.Copy).then_inc(xT_hi_made, 1)
                        sum_square(b + 3, j, slot, 1 - slot)
                magnitude(C - 1)

            step(0, 0, 0, True, True, first=True)
            step(1, 0, 1, True, True)
            with act.Fori(1, NB // 2 - 1) as pair:
                for slot in range(2):
                    step(pair * 2 + slot, pair, slot, True, True)
            step(NB - 2, NB // 2 - 1, 0, True, False)
            step(NB - 1, NB // 2 - 1, 1, False, False)

        @block.tensor
        def _(pe):
            def project_part(o, c, j, rhs_hi, rhs_lo):
                cols = slice(j * P, (j + 1) * P)
                nc.tensor.matmul(o, gs_hi[:, c, cols], rhs_hi[:, c, :], start=(c == 0), stop=False)
                nc.tensor.matmul(o, gs_hi[:, c, cols], rhs_lo[:, c, :], start=False, stop=False)
                return nc.tensor.matmul(o, gs_lo[:, c, cols], rhs_hi[:, c, :], start=False, stop=(c == C - 1))

            def project(j, bank):
                for c in range(C):
                    last = project_part(bank[:, :], c, j, xT_hi, xT_lo)
                last.then_inc(project_done, 1)

            def product(o, left_hi, left_lo, right_hi, right_lo):
                for c in range(C):
                    nc.tensor.matmul(o, left_hi[c], right_hi[:, c, :], start=(c == 0), stop=False)
                    nc.tensor.matmul(o, left_hi[c], right_lo[:, c, :], start=False, stop=False)
                    last = nc.tensor.matmul(o, left_lo[c], right_hi[:, c, :], start=False, stop=(c == C - 1))
                return last

            for c in range(C):
                pe.wait_ge(gs_lo_made, c + 1)
                pe.wait_ge(wT_lo_made, c + 1)
                for j in range(C):
                    last = project_part(token_ps[j][:, :], c, j, zT_hi, zT_lo)
                    if c == C - 1:
                        last.then_inc(project_done, 1)
            pe.wait_ge(xT_lo_made, C)
            for j in range(C):
                project(j, (project_ps + turn_ps)[j])
            pe.wait_ge(ident_made, 2)
            pe.wait_ge(W_made, C)

            def step(b, more, first=False):
                pe.wait_ge(F_made, C * (b + 1))
                for j in range(C):
                    pe.wait_ge(square_done, 2 * C * b + SQUARE_CREDIT - C + j + 1)
                    cols = slice(j * P, (j + 1) * P)
                    product(token_ps[j][:, :], [F_hi[:, c, cols] for c in range(C)], [F_lo[:, c, cols] for c in range(C)],
                            W_hi, W_lo).then_inc(mix_done, 1)

                def turn(j):
                    pe.wait_ge(z_made, C * b + j + 1)
                    pe.wait_ge(zT_made, C * b + j - 1 + TURN_CREDIT)
                    for c in range(C):
                        last = nc.tensor.transpose(turn_ps[j % 2][:, c * P:(c + 1) * P], z[:, j, c * P:(c + 1) * P], ident[:, :])
                    last.then_inc(turn_done, 1)

                def phase(j):
                    pe.wait_ge(zT_made, C * b + j + 1 + TURN_CREDIT)
                    for part, (hi, lo) in enumerate(((cos_hi, cos_lo), (sin_hi, sin_lo))):
                        use = 2 * j + part
                        if use < 4:
                            pe.wait_ge(y_made, C * b + use + 1)
                        else:
                            pe.wait_ge(square_done, 2 * C * b + SQUARE_CREDIT + use - 3)
                        if first and j == 0:
                            pe.wait_ge(trig_made, C * (part + 1))
                        cols = [slice(c * P, (c + 1) * P) for c in range(C)]
                        product(token_ps[use % 4][:, :], [zT_hi[:, j, s] for s in cols], [zT_lo[:, j, s] for s in cols],
                                hi, lo).then_inc(phase_done, 1)

                if more:
                    pe.wait_ge(xT_lo_made, C * (b + 2))
                    for j in range(C):
                        pe.wait_ge(expo_made, C * (b + 2) + j - 1)
                        project(j, project_ps[j % 2])
                        turn(j)
                    for j in range(C):
                        phase(j)
                else:
                    turn(0)
                    turn(1)
                    phase(0)
                    turn(2)
                    turn(3)
                    for j in range(1, C):
                        phase(j)

            step(0, True, first=True)
            with pe.Fori(1, NB - 1) as b:
                step(b, True)
            step(NB - 1, False)

        @block.vector
        def _(dve):
            dve.sem_inc(zT_made, TURN_CREDIT)
            tt, ts, stt = nc.vector.tensor_tensor, nc.vector.tensor_scalar, nc.vector.scalar_tensor_tensor

            def lower(dst, whole, hi):
                return tt(dst, whole, hi.bitcast(F32), ALU.subtract)

            def exponent(q, j, k, bank):
                dve.wait_ge(project_done, C * q + j + 1)
                stt(out=expo[:, j % 2, :], in0=norm_bc[:, k, :], scalar=neg_half_ab[:, j:j + 1],
                    in1=bank[:, :], op0=ALU.mult, op1=ALU.add).then_inc(expo_made, 1)

            def split_features(b, j):
                dve.wait_ge(exp_done, 2 * (C * (b + 1) + j + 1))
                lower(F_lo[:, j, :], F_raw[:, j % 2, :], F_hi[:, j, :]).then_inc(F_made, 1)

            def split_lo(b, c):
                dve.wait_ge(xT_hi_made, C * b + c + 1)
                lower(xT_lo[:, c, :], xT_raw[:, c, :], xT_hi[:, c, :]).then_inc(xT_lo_made, 1)

            for c in range(C):
                dve.wait_ge(gs_hi_made, c + 1)
                lower(gs_lo[:, c, :], trig[:, c, :], gs_hi[:, c, :]).then_inc(gs_lo_made, 1)
                dve.wait_ge(wT_hi_made, c + 1)
                lower(zT_lo[:, c, :], z[:, c, :], zT_hi[:, c, :]).then_inc(wT_lo_made, 1)
            dve.wait_ge(xis_loaded, 16)
            ts(neg_half_ab[:, :], ab[:, :], -0.5, None, ALU.mult).then_inc(half_ab_made, 1)
            dve.wait_ge(AB_made, 1)
            stt(out=W_scale[:, :], in0=AB[:, :], scalar=1.0 / R, in1=AB[:, :],
                op0=ALU.mult, op1=ALU.mult).then_inc(W_scale_made, 1)
            dve.wait_ge(half_ab_made, 1)
            dve.wait_ge(W_scale_made, 1)

            def scale_W(j):
                dve.wait_ge(exp_done, 2 * (j + 1))
                ts(W_hi[:, j, :], F_raw[:, j % 2, :], W_scale[:, j:j + 1], None, ALU.mult).then_inc(W_hi_made, 1)
                dve.wait_ge(W_hi_made, j + 1)
                stt(out=W_lo[:, j, :], in0=F_raw[:, j % 2, :], scalar=W_scale[:, j:j + 1],
                    in1=W_hi[:, j, :].bitcast(F32), op0=ALU.mult, op1=ALU.subtract).then_inc(W_made, 1)

            dve.wait_ge(norms_loaded, 16)
            exponent(0, 0, 0, token_ps[0])
            for j in range(1, C):
                exponent(0, j, 0, token_ps[j])
                scale_W(j - 1)
            dve.wait_ge(norms_loaded, 32)
            exponent(1, 0, 1, project_ps[0])
            scale_W(C - 1)
            for j in range(1, C):
                exponent(1, j, 1, (project_ps + turn_ps)[j])
                split_features(0, j - 1)
            split_features(0, C - 1)

            steps = 0
            def reduce_angles(buf, chunks, n):
                nonlocal steps
                for part in (TWO_PI_A, TWO_PI_B):
                    for i, c in enumerate(chunks):
                        if part == TWO_PI_A:
                            dve.wait_ge(turns_made, n + c + 1)
                        else:
                            dve.wait_ge(angle_step, steps - len(chunks) + 1)
                        stt(out=buf[:, c, :], in0=buf[:, C + c, :], scalar=-part, in1=buf[:, c, :],
                            op0=ALU.mult, op1=ALU.add).then_inc(angle_step, 1)
                        steps += 1
                for i, c in enumerate(chunks):
                    dve.wait_ge(angle_step, steps - len(chunks) + i + 1)
                    ts(buf[:, c, :], buf[:, c, :], PI_INSIDE, -PI_INSIDE, ALU.min, ALU.max).then_inc(angle_made, 1)

            def split_sines(buf, hi, lo, n):
                for c in range(C):
                    dve.wait_ge(sine_made, 2 * (n + c + 1))
                    lower(lo[:, c, :], buf[:, C + c, :], hi[:, c, :]).then_inc(trig_made, 1)

            reduce_angles(trig, (0, 1), 0)
            reduce_angles(trig, (2, 3), 0)
            for c in range(C):
                split_lo(1, c)
            split_sines(trig, cos_hi, cos_lo, 0)

            def halves(n, j, src, src_made, st, st_made):
                dve.wait_ge(src_made, n)
                nc.vector.bn_stats(st[:, j, :], src).then_inc(st_made, 1)

            def moments(j, st, m, m_made):
                nc.vector.bn_aggr(m[:, j, :], st[:, j, :]).then_inc(m_made, 1)

            def normalise(n, j, dst, src, root_made, m, root, dst_made):
                dve.wait_ge(root_made, n)
                ts(dst, src, m[:, j, 0:1], root[:, j:j + 1], ALU.subtract, ALU.mult).then_inc(dst_made, 1)

            def step(b, pair, slot, more, ahead, first=False):
                n = [C * b + j + 1 for j in range(C)]
                dve.wait_ge(x_loaded[slot], 16 * (pair + 1 + slot))

                def residual1(j):
                    if j >= 2:
                        dve.wait_ge(z_made, n[j - 2])
                    dve.wait_ge(mix_done, n[j])
                    tt(y[:, j % 2, :], token_ps[j][:, :], x_tok[:, slot, j, :], ALU.add).then_inc(y_made, 1)

                def norm1(j):
                    normalise(n[j], j, z[:, j, :], y[:, j % 2, :], rstd_made, mv, rstd, z_made)

                for j in range(C):
                    if j == 1:
                        dve.wait_ge(stats_made, n[0])
                    residual1(j)
                    if j == 1:
                        moments(0, stats, mv, mv_made)
                    halves(n[j], j, y[:, j % 2, :], y_made, stats, stats_made)
                    if j >= 1:
                        dve.wait_ge(stats_made, n[j])
                        norm1(j - 1)
                        moments(j, stats, mv, mv_made)
                    if more and j == C - 1:
                        dve.wait_ge(norms_loaded, 16 * (b + 3))
                        exponent(b + 2, 0, slot, project_ps[0])
                norm1(C - 1)

                for j in range(C):
                    if more and j >= 1:
                        exponent(b + 2, j, slot, project_ps[j % 2])
                    dve.wait_ge(zT_hi_made, n[j])
                    lower(zT_lo[:, j, :], turn_ps[j % 2][:, :], zT_hi[:, j, :]).then_inc(zT_made, 1)
                    if more:
                        split_features(b + 1, j)
                    if first:
                        reduce_angles(late, (j,), C)
                if first:
                    split_sines(late, sin_hi, sin_lo, C)

                def residual2(j):
                    if j >= 2:
                        dve.wait_ge(out_made, n[j - 2])
                    dve.wait_ge(mag_made, n[j])
                    tt(y2[:, j % 2, :], z[:, j, :], mag[:, j % 2, :], ALU.add).then_inc(y2_made, 1)
                    halves(n[j], j, y2[:, j % 2, :], y2_made, stats2, stats2_made)
                    dve.wait_ge(stats2_made, n[j])

                def norm2(j):
                    dve.wait_ge(out_stored[j % 2], 32 * b + 16 * (j // 2) + STORE_CREDIT)
                    normalise(n[j], j, o_tile[:, j % 2, :], y2[:, j % 2, :], rstd2_made, mv2, rstd2, out_made)

                for j in range(C):
                    if j >= 1:
                        residual2(j - 1)
                    if ahead:
                        split_lo(b + 2, j)
                    if j >= 1:
                        moments(j - 1, stats2, mv2, mv2_made)
                    if j >= 2:
                        norm2(j - 2)
                    dve.wait_ge(square_done, 2 * C * b + 2 * j + 2 + SQUARE_CREDIT)
                    tt(re2[:, j % 2, :], re2[:, j % 2, :], im2[:, j % 2, :], ALU.add).then_inc(sum_made, 1)
                residual2(C - 1)
                norm2(C - 2)
                moments(C - 1, stats2, mv2, mv2_made)
                norm2(C - 1)

            step(0, 0, 0, True, True, first=True)
            step(1, 0, 1, True, True)
            with dve.Fori(1, NB // 2 - 1) as pair:
                for slot in range(2):
                    step(pair * 2 + slot, pair, slot, True, True)
            step(NB - 2, NB // 2 - 1, 0, True, False)
            step(NB - 1, NB // 2 - 1, 1, False, False)


def kernel(**inputs):
    import concourse.bacc as _bacc
    from concourse.bass_utils import run_bass_kernel_spmd as _run

    x = np.asarray(inputs["L0_attn_x"])
    tokens = x.reshape(-1, x.shape[-1])
    w = np.asarray(inputs["L0_attn_input_weights"])
    gs = np.asarray(inputs["L0_attn_proj_matrix"])
    laid = {
        "xT": tokens.T, "x": tokens, "wT": w.T, "w": w, "xis": inputs["L0_attn_xis"], "gsT": gs.T,
        "theta": inputs["L0_ffn_theta"], "phi": inputs["L0_ffn_phi"],
        "theta_noise": inputs["L0_ffn_theta_noise"], "phi_noise": inputs["L0_ffn_phi_noise"],
    }
    nc = _bacc.Bacc("TRN2", target_bir_lowering=False, num_devices=1)
    arrays, args = {}, []
    for name, a in laid.items():
        a = np.ascontiguousarray(a)
        arrays[f"in_{name}"] = a
        args.append(nc.dram_tensor(f"in_{name}", a.shape, mybir.dt.from_np(a.dtype), kind="ExternalInput").ap())
    args.append(nc.dram_tensor("out_tokens", tokens.shape, F32, kind="ExternalOutput").ap())
    build(nc, *args)
    r = _run(nc, [arrays], core_ids=[0])
    return r.results[0]["out_tokens"].reshape(x.shape)
```

```python
from contextlib import ExitStack

import numpy as np

import concourse.bass as bass
from concourse import mybir

P = 128
ALU = mybir.AluOpType
ACT = mybir.ActivationFunctionType
F32 = mybir.dt.float32
F32R = mybir.dt.float32r

EPS = 1e-5
TWO_PI_A = 6.28125
TWO_PI_B = float(np.float32(2 * np.pi - TWO_PI_A))
ROUNDER = 1.5 * 2.0**23
PI_INSIDE = float(np.nextafter(np.float32(np.pi), np.float32(0)))
HALF_PI = float(np.float32(np.pi / 2))


def build(nc, xT, x, wT, w, xis, gsT, theta, phi, theta_noise, phi_noise, out):
    T, D = x.shape
    R = gsT.shape[1]
    O = w.shape[0]
    B = 512
    NB = T // B
    C = D // P
    assert D == R == O == B == C * P and T % (2 * B) == 0 and NB >= 4

    xT_blocks = xT.rearrange("(c p) (b t) -> b p c t", p=P, t=B)
    x_blocks = x.rearrange("(b c p) d -> b p c d", p=P, c=C)
    out_tiles = out.rearrange("(b c p) d -> b c p d", p=P, c=C)
    by_chunk = lambda m: m.rearrange("(c p) n -> p c n", p=P)
    norms_dram = [nc.dram_tensor(f"token_norms_{k}", (B,), F32, kind="Internal").ap() for k in range(2)]

    with ExitStack() as ctx:
        sb = lambda name, shape, dt=F32: ctx.enter_context(nc.sbuf_tensor(name, shape, dt))
        bank = lambda name: ctx.enter_context(nc.psum_tensor(name, [P, 512], F32))
        sem = lambda name: ctx.enter_context(nc.semaphore(name))

        gs_hi, gs_lo = sb("gs_hi", [P, C, R], F32R), sb("gs_lo", [P, C, R], F32R)
        W_hi, W_lo = sb("W_hi", [P, C, O], F32R), sb("W_lo", [P, C, O], F32R)
        cos_hi, cos_lo = sb("cos_hi", [P, C, O], F32R), sb("cos_lo", [P, C, O], F32R)
        sin_hi, sin_lo = sb("sin_hi", [P, C, O], F32R), sb("sin_lo", [P, C, O], F32R)
        xT_raw = sb("xT_raw", [P, C, B])
        xT_hi, xT_lo = sb("xT_hi", [P, C, B], F32R), sb("xT_lo", [P, C, B], F32R)
        x_tok = sb("x_tok", [P, 2, C, D])
        F_hi, F_lo = sb("F_hi", [P, C, B], F32R), sb("F_lo", [P, C, B], F32R)
        z = sb("z", [P, C, D])
        zT_hi, zT_lo = sb("zT_hi", [P, C, D], F32R), sb("zT_lo", [P, C, D], F32R)
        norm_bc = sb("norm_bc", [P, 2, B])
        expo = sb("expo", [P, 2, B])
        F_raw = sb("F_raw", [P, 2, B])
        y = sb("y", [P, 2, D])
        late = sb("late", [P, 8, D])
        re2, im2, mag, y2 = late[:, 0:2], late[:, 2:4], late[:, 4:6], late[:, 6:8]
        o_tile = sb("o_tile", [P, 2, D])
        unused = sb("unused", [P, D])
        trig = sb("trig", [P, 8, D])
        ab = sb("ab", [P, C])
        neg_half_ab = sb("neg_half_ab", [P, C])
        AB = sb("AB", [P, C])
        W_scale = sb("W_scale", [P, C])
        norm_col = sb("norm_col", [P, 2, C])
        stats = sb("stats", [P, C, 6])
        mv = sb("mv", [P, C, 2])
        var_eps = sb("var_eps", [P, C])
        rstd = sb("rstd", [P, C])
        stats2 = sb("stats2", [P, C, 6])
        mv2 = sb("mv2", [P, C, 2])
        var_eps2 = sb("var_eps2", [P, C])
        rstd2 = sb("rstd2", [P, C])
        neg_half = sb("neg_half", [P, 1])
        eps = sb("eps", [P, 1])
        ident = sb("ident", [P, P])

        project_ps = [bank(f"project_ps{k}") for k in range(2)]
        turn_ps = [bank(f"turn_ps{k}") for k in range(2)]
        token_ps = [bank(f"token_ps{k}") for k in range(4)]

        xis_loaded = sem("xis_loaded")
        gs_loaded = [sem(f"gs_loaded_{c}") for c in range(C)]
        wT_loaded = [sem(f"wT_loaded_{c}") for c in range(C)]
        theta_loaded = [sem(f"theta_loaded_{c}") for c in range(C)]
        phi_loaded = [sem(f"phi_loaded_{c}") for c in range(C)]
        xT_loaded = sem("xT_loaded")
        x_loaded = [sem("x_loaded_even"), sem("x_loaded_odd")]
        norms_stored, norms_loaded = sem("norms_stored"), sem("norms_loaded")
        out_stored = [sem("out_stored_0"), sem("out_stored_1")]
        ident_made, exponent_set, half_ab_made = sem("ident_made"), sem("exponent_set"), sem("half_ab_made")
        gs_hi_made, gs_lo_made = sem("gs_hi_made"), sem("gs_lo_made")
        wT_hi_made, wT_lo_made = sem("wT_hi_made"), sem("wT_lo_made")
        AB_made, W_scale_made = sem("AB_made"), sem("W_scale_made")
        W_hi_made, W_made = sem("W_hi_made"), sem("W_made")
        trig_step, turns_made = sem("trig_step"), sem("turns_made")
        angle_step, angle_made = sem("angle_step"), sem("angle_made")
        sine_made = sem("sine_made")
        cos_made = [sem("cos_made_front"), sem("cos_made_back")]
        sin_made = [sem("sin_made_front"), sem("sin_made_back")]
        sumsq_done = sem("sumsq_done")
        xT_hi_made, xT_lo_made = sem("xT_hi_made"), sem("xT_lo_made")
        project_done, expo_made, exp_done, F_made = sem("project_done"), sem("expo_made"), sem("exp_done"), sem("F_made")
        mix_done, y_made, stats_made, mv_made = sem("mix_done"), sem("y_made"), sem("stats_made"), sem("mv_made")
        var_made, rstd_made, z_made = sem("var_made"), sem("rstd_made"), sem("z_made")
        turn_done, zT_hi_made, zT_made = sem("turn_done"), sem("zT_hi_made"), sem("zT_made")
        phase_done, square_done, sum_made, mag_made = sem("phase_done"), sem("square_done"), sem("sum_made"), sem("mag_made")
        y2_made, stats2_made, mv2_made = sem("y2_made"), sem("stats2_made"), sem("mv2_made")
        var2_made, rstd2_made, out_made = sem("var2_made"), sem("rstd2_made"), sem("out_made")

        TURN_CREDIT = 2
        SQUARE_CREDIT = 2 * C
        STORE_CREDIT = 16

        PHASE_ORDER = [(j, part) for j in range(C) for part in range(2)]
        PHASE_ORDER_FIRST = [(0, 0), (1, 0), (0, 1), (1, 1)] + PHASE_ORDER[4:]

        block = ctx.enter_context(nc.Block())


        @block.sync
        def _(sp):
            def store_norms(q, k):
                sp.wait_ge(sumsq_done, C * (q + 1))
                sp.dma_start(norms_dram[k].rearrange("(c p) -> p c", p=P), norm_col[:, k, :],
                             allow_slow_non_contiguous=True).then_inc(norms_stored, 16)

            def fetch_norms(q, k):
                sp.wait_ge(norms_stored, 16 * (q + 1))
                sp.dma_start(norm_bc[:, k, :], norms_dram[k].partition_broadcast(P)).then_inc(norms_loaded, 16)

            def turn_norms(q, k):
                store_norms(q, k)
                fetch_norms(q, k)

            def load_theta(c):
                sp.dma_start(trig[:, C + c, :], by_chunk(theta_noise)[:, c, :]).then_inc(theta_loaded[c], 16)
                sp.wait_ge(gs_lo_made, c + 1)
                sp.dma_start(trig[:, c, :], by_chunk(theta)[:, c, :]).then_inc(theta_loaded[c], 16)

            def store_out(b, j):
                sp.wait_ge(out_made, C * b + j + 1)
                sp.dma_start(out_tiles[b][j], o_tile[:, j % 2, :]).then_inc(out_stored[j % 2], 16)

            sp.sem_inc(out_stored[0], STORE_CREDIT)
            sp.sem_inc(out_stored[1], STORE_CREDIT)
            for c in range(C):
                sp.dma_start(trig[:, c, :], by_chunk(gsT)[:, c, :]).then_inc(gs_loaded[c], 16)
                sp.dma_start(z[:, c, :], by_chunk(wT)[:, c, :]).then_inc(wT_loaded[c], 16)
            sp.dma_start(ab[:, :], xis.rearrange("(c p) -> p c", p=P),
                         allow_slow_non_contiguous=True).then_inc(xis_loaded, 16)
            sp.dma_start(x_tok[:, 1], by_chunk(w)).then_inc(x_loaded[1], 16)
            sp.dma_start(xT_raw[:, :, :], xT_blocks[0]).then_inc(xT_loaded, 16)
            sp.dma_start(x_tok[:, 0], x_blocks[0]).then_inc(x_loaded[0], 16)
            store_norms(0, 0)
            load_theta(0)
            fetch_norms(0, 0)
            load_theta(1)
            store_norms(1, 1)
            load_theta(2)
            sp.wait_ge(norms_loaded, 16)
            fetch_norms(1, 1)
            load_theta(3)
            sp.wait_ge(xT_lo_made, C)
            sp.dma_start(xT_raw[:, :, :], xT_blocks[1]).then_inc(xT_loaded, 16)
            sp.dma_start(x_tok[:, 1], x_blocks[1]).then_inc(x_loaded[1], 16)
            for c in range(C):
                sp.dma_start(late[:, c, :], by_chunk(phi)[:, c, :]).then_inc(phi_loaded[c], 16)
                sp.dma_start(late[:, C + c, :], by_chunk(phi_noise)[:, c, :]).then_inc(phi_loaded[c], 16)
            sp.wait_ge(norms_loaded, 32)
            sp.wait_ge(expo_made, C)
            turn_norms(2, 0)

            def step(b, slot, ahead):
                if ahead:
                    sp.wait_ge(xT_lo_made, C * (b + 2))
                    sp.dma_start(xT_raw[:, :, :], xT_blocks[b + 2]).then_inc(xT_loaded, 16)
                    sp.wait_ge(y_made, C * (b + 1))
                    sp.dma_start(x_tok[:, slot], x_blocks[b + 2]).then_inc(x_loaded[slot], 16)
                for j in range(C):
                    if ahead and j == 2:
                        sp.wait_ge(expo_made, C * (b + 3))
                        turn_norms(b + 3, 1 - slot)
                    store_out(b, j)

            with sp.Fori(0, NB // 2 - 1) as pair:
                for slot in range(2):
                    step(pair * 2 + slot, slot, True)
            for slot in range(2):
                step(NB - 2 + slot, slot, False)
            for k in range(2):
                sp.wait_ge(out_stored[k], STORE_CREDIT + 16 * NB * C // 2)

        @block.gpsimd
        def _(pool):
            pool.memset(neg_half[:, :], -0.5).then_inc(exponent_set, 1)
            pool.memset(eps[:, :], EPS).then_inc(exponent_set, 1)
            pool.memset(ident[:, :], 0.0).then_inc(ident_made, 1)
            pool.wait_ge(ident_made, 1)
            pool.affine_select(out=ident[:, :], in_=ident[:, :], compare_op=ALU.not_equal, fill=1.0,
                               base=0, pattern=[[-1, P]], channel_multiplier=1).then_inc(ident_made, 1)

            steps = 0
            def count_turns(buf, c, shift, take=False):
                nonlocal steps
                angle, turns = buf[:, c, :], buf[:, C + c, :]
                pool.tensor_tensor(angle, angle, turns, ALU.add).then_inc(trig_step, 1)
                steps += 1
                pool.wait_ge(trig_step, steps)
                if shift:
                    pool.tensor_scalar(angle, angle, shift, 1.0, ALU.add, ALU.mult).then_inc(trig_step, 1)
                    steps += 1
                    pool.wait_ge(trig_step, steps)
                pool.tensor_scalar(turns, angle, 1.0 / (2 * np.pi), ROUNDER, ALU.mult, ALU.add).then_inc(trig_step, 1)
                steps += 1
                pool.wait_ge(trig_step, steps)
                if not take:
                    pool.tensor_scalar(turns, turns, -ROUNDER, 1.0, ALU.add, ALU.mult).then_inc(turns_made, 1)
                    return
                pool.tensor_scalar(turns, turns, -ROUNDER, -TWO_PI_A, ALU.add, ALU.mult).then_inc(trig_step, 1)
                steps += 1
                pool.wait_ge(trig_step, steps)
                pool.tensor_tensor(angle, angle, turns, ALU.add).then_inc(turns_made, 1)

            for c in range(C):
                pool.wait_ge(theta_loaded[c], 32)
                count_turns(trig, c, HALF_PI, take=(c >= 2))
            for c in (0, 1):
                pool.wait_ge(phi_loaded[c], 32)
                count_turns(late, c, 0.0)

            def lower_sine(buf, c, hi, lo, n, made):
                pool.wait_ge(sine_made, 2 * (n + c + 1))
                pool.tensor_tensor(lo[:, c, :], buf[:, C + c, :], hi[:, c, :].bitcast(F32), ALU.subtract).then_inc(made, 1)

            def inverse_root(b, j, mv_ready, moments, shifted, shifted_made, root, root_made):
                n = C * b + j + 1
                pool.wait_ge(mv_ready, n)
                pool.tensor_tensor(shifted[:, j:j + 1], moments[:, j, 1:2], eps[:, :], ALU.add).then_inc(shifted_made, 1)
                pool.wait_ge(shifted_made, n)
                pool.tensor_tensor(root[:, j:j + 1], shifted[:, j:j + 1], neg_half[:, :], ALU.pow).then_inc(root_made, 1)

            def last_inverse_root2(b):
                inverse_root(b, C - 1, mv2_made, mv2, var_eps2, var2_made, rstd2, rstd2_made)

            def step(b, first=False):
                for j in range(C):
                    inverse_root(b, j, mv_made, mv, var_eps, var_made, rstd, rstd_made)
                    if not first and j == 0:
                        last_inverse_root2(b - 1)
                    if first and j == 1:
                        lower_sine(trig, 0, cos_hi, cos_lo, 0, cos_made[0])
                if first:
                    lower_sine(trig, 1, cos_hi, cos_lo, 0, cos_made[0])
                    for c in (2, 3):
                        pool.wait_ge(phi_loaded[c], 32)
                        count_turns(late, c, 0.0, take=True)
                    for c in (0, 1):
                        lower_sine(late, c, sin_hi, sin_lo, C, sin_made[0])
                for j in range(C - 1):
                    inverse_root(b, j, mv2_made, mv2, var_eps2, var2_made, rstd2, rstd2_made)

            pool.wait_ge(exponent_set, 2)
            step(0, first=True)
            with pool.Fori(1, NB) as b:
                step(b)
            last_inverse_root2(NB - 1)

        @block.scalar
        def _(act):
            act.sem_inc(square_done, SQUARE_CREDIT)
            def sum_square(q, j, slot, k):
                if not (isinstance(q, int) and C * q + j == 0):
                    act.wait_ge(sumsq_done, C * q + j)
                nc.scalar.activation(unused[:, :], x_tok[:, slot, j, :], ACT.Square,
                                     accum_out=norm_col[:, k, j:j + 1]).then_inc(sumsq_done, 1)

            def sum_squares(q, slot):
                for j in range(C):
                    sum_square(q, j, slot, q % 2)

            def split_hi(b):
                act.wait_ge(xT_loaded, 16 * (b + 1))
                for c in range(C):
                    nc.scalar.activation(xT_hi[:, c, :], xT_raw[:, c, :], ACT.Copy).then_inc(xT_hi_made, 1)

            for c in range(C):
                act.wait_ge(gs_loaded[c], 16)
                nc.scalar.activation(gs_hi[:, c, :], trig[:, c, :], ACT.Copy).then_inc(gs_hi_made, 1)
                act.wait_ge(wT_loaded[c], 16)
                nc.scalar.activation(zT_hi[:, c, :], z[:, c, :], ACT.Copy).then_inc(wT_hi_made, 1)
            act.wait_ge(x_loaded[1], 16)
            sum_squares(0, 1)
            split_hi(0)
            act.wait_ge(xis_loaded, 16)
            nc.scalar.activation(AB[:, :], ab[:, :], ACT.Exp).then_inc(AB_made, 1)
            act.wait_ge(x_loaded[0], 16)
            sum_squares(1, 0)
            for j in range(C):
                act.wait_ge(expo_made, j + 1)
                if j >= 2:
                    act.wait_ge(W_made, j - 1)
                nc.scalar.activation(F_raw[:, j % 2, :], expo[:, j % 2, :], ACT.Exp,
                                     scale=ab[:, j:j + 1]).then_inc(exp_done, 2)
                act.wait_ge(exp_done, 2 * (j + 1))
                if j == 0:
                    act.wait_ge(W_scale_made, 1)
                nc.scalar.activation(W_hi[:, j, :], F_raw[:, j % 2, :], ACT.Copy,
                                     scale=W_scale[:, j:j + 1]).then_inc(W_hi_made, 1)

            def features(q, j):
                act.wait_ge(expo_made, C * q + j + 1)
                nc.scalar.activation(F_hi[:, j, :], expo[:, j % 2, :], ACT.Exp,
                                     scale=ab[:, j:j + 1]).then_inc(exp_done, 1)
                nc.scalar.activation(F_raw[:, j % 2, :], expo[:, j % 2, :], ACT.Exp,
                                     scale=ab[:, j:j + 1]).then_inc(exp_done, 1)

            for j in range(C):
                features(1, j)
            act.wait_ge(project_done, 2 * C)
            split_hi(1)
            act.wait_ge(x_loaded[1], 32)
            sum_squares(2, 1)

            def sine(buf, c, hi, n):
                act.wait_ge(angle_made, n + c + 1)
                nc.scalar.activation(hi[:, c, :], buf[:, c, :], ACT.Sin).then_inc(sine_made, 1)
                nc.scalar.activation(buf[:, C + c, :], buf[:, c, :], ACT.Sin).then_inc(sine_made, 1)

            for c in (0, 1):
                sine(trig, c, cos_hi, 0)

            def step(b, pair, slot, more, ahead, first=False):
                def round_turned(j):
                    act.wait_ge(turn_done, C * b + j + 1)
                    nc.scalar.activation(zT_hi[:, j, :], turn_ps[j % 2][:, :], ACT.Copy).then_inc(zT_hi_made, 1)

                def square(j, part):
                    order = PHASE_ORDER_FIRST if first else PHASE_ORDER
                    act.wait_ge(phase_done, 2 * C * b + order.index((j, part)) + 1)
                    nc.scalar.activation((re2, im2)[part][:, j % 2, :], token_ps[(2 * j + part) % 4][:, :],
                                         ACT.Square).then_inc(square_done, 1)

                if first:
                    round_turned(0)
                    round_turned(1)
                    sine(trig, 2, cos_hi, 0)
                    sine(trig, 3, cos_hi, 0)
                    round_turned(2)
                    round_turned(3)
                    sine(late, 0, sin_hi, C)
                    sine(late, 1, sin_hi, C)
                    sine(late, 2, sin_hi, C)
                    sine(late, 3, sin_hi, C)
                    act.wait_ge(sine_made, 4 * C)
                    square(0, 0)
                    for j in range(C):
                        if j >= 2:
                            act.wait_ge(F_made, C + j - 1)
                        features(b + 2, j)
                        if j >= 1:
                            square(*((0, 1), (1, 0), (1, 1))[j - 1])
                else:
                    for j in range(C):
                        round_turned(j)
                        if more:
                            features(b + 2, j)

                def magnitude(j):
                    act.wait_ge(sum_made, C * b + j + 1)
                    nc.scalar.activation(mag[:, j % 2, :], re2[:, j % 2, :], ACT.Sqrt).then_inc(mag_made, 1)

                if ahead:
                    act.wait_ge(xT_loaded, 16 * (b + 3))
                    act.wait_ge(x_loaded[slot], 16 * (pair + 2 + slot))
                for j in range(C):
                    if j >= 2:
                        act.wait_ge(mag_made, C * b + j - 1)
                    for part in range(2):
                        if not (first and j < 2):
                            square(j, part)
                        if part == 0 and j >= 1 and not (first and j == 2):
                            magnitude(j - 1)
                    if first and j == 1:
                        magnitude(1)
                    if ahead:
                        nc.scalar.activation(xT_hi[:, j, :], xT_raw[:, j, :], ACT.Copy).then_inc(xT_hi_made, 1)
                        sum_square(b + 3, j, slot, 1 - slot)
                magnitude(C - 1)

            step(0, 0, 0, True, True, first=True)
            step(1, 0, 1, True, True)
            with act.Fori(1, NB // 2 - 1) as pair:
                for slot in range(2):
                    step(pair * 2 + slot, pair, slot, True, True)
            step(NB - 2, NB // 2 - 1, 0, True, False)
            step(NB - 1, NB // 2 - 1, 1, False, False)

        @block.tensor
        def _(pe):
            def project_part(o, c, j, rhs_hi, rhs_lo):
                cols = slice(j * P, (j + 1) * P)
                nc.tensor.matmul(o, gs_hi[:, c, cols], rhs_hi[:, c, :], start=(c == 0), stop=False)
                nc.tensor.matmul(o, gs_hi[:, c, cols], rhs_lo[:, c, :], start=False, stop=False)
                return nc.tensor.matmul(o, gs_lo[:, c, cols], rhs_hi[:, c, :], start=False, stop=(c == C - 1))

            def project(j, bank):
                for c in range(C):
                    last = project_part(bank[:, :], c, j, xT_hi, xT_lo)
                last.then_inc(project_done, 1)

            def product(o, left_hi, left_lo, right_hi, right_lo, made=None):
                for c in range(C):
                    if made:
                        pe.wait_ge(made[c // 2], c % 2 + 1)
                    nc.tensor.matmul(o, left_hi[c], right_hi[:, c, :], start=(c == 0), stop=False)
                    nc.tensor.matmul(o, left_hi[c], right_lo[:, c, :], start=False, stop=False)
                    last = nc.tensor.matmul(o, left_lo[c], right_hi[:, c, :], start=False, stop=(c == C - 1))
                return last

            for c in range(C):
                pe.wait_ge(gs_lo_made, c + 1)
                pe.wait_ge(wT_lo_made, c + 1)
                for j in range(C):
                    last = project_part(token_ps[j][:, :], c, j, zT_hi, zT_lo)
                    if c == C - 1:
                        last.then_inc(project_done, 1)
            pe.wait_ge(xT_lo_made, C)
            for j in range(C):
                project(j, (project_ps + turn_ps)[j])
            pe.wait_ge(ident_made, 2)
            pe.wait_ge(W_made, C)

            def step(b, more, first=False):
                def mix_part(j, c):
                    cols = slice(j * P, (j + 1) * P)
                    o = token_ps[j][:, :]
                    nc.tensor.matmul(o, F_hi[:, c, cols], W_hi[:, c, :], start=(c == 0), stop=False)
                    nc.tensor.matmul(o, F_hi[:, c, cols], W_lo[:, c, :], start=False, stop=False)
                    return nc.tensor.matmul(o, F_lo[:, c, cols], W_hi[:, c, :], start=False, stop=(c == C - 1))

                def turn(j):
                    pe.wait_ge(z_made, C * b + j + 1)
                    pe.wait_ge(zT_made, C * b + j - 1 + TURN_CREDIT)
                    for c in range(C):
                        last = nc.tensor.transpose(turn_ps[j % 2][:, c * P:(c + 1) * P], z[:, j, c * P:(c + 1) * P], ident[:, :])
                    last.then_inc(turn_done, 1)

                if first:
                    for c in range(C // 2):
                        pe.wait_ge(F_made, c + 1)
                        for j in range(C):
                            mix_part(j, c)
                    pe.wait_ge(F_made, C)
                else:
                    pe.wait_ge(F_made, C * (b + 1))
                for j in range(C):
                    pe.wait_ge(square_done, 2 * C * b + SQUARE_CREDIT - C + j + 1)
                    for c in range(C // 2 if first else 0, C):
                        last = mix_part(j, c)
                    last.then_inc(mix_done, 1)
                    if not more and j == C - 2:
                        turn(0)

                def phase(j, part):
                    hi, lo = ((cos_hi, cos_lo), (sin_hi, sin_lo))[part]
                    use = 2 * j + part
                    pe.wait_ge(zT_made, C * b + j + 1 + TURN_CREDIT)
                    if use < 4:
                        pe.wait_ge(y_made, C * b + use + 1)
                    else:
                        pe.wait_ge(square_done, 2 * C * b + SQUARE_CREDIT + use - 3)
                    cols = [slice(c * P, (c + 1) * P) for c in range(C)]
                    made = (cos_made, sin_made)[part] if first and j == 0 else None
                    product(token_ps[use % 4][:, :], [zT_hi[:, j, s] for s in cols], [zT_lo[:, j, s] for s in cols],
                            hi, lo, made).then_inc(phase_done, 1)

                if more:
                    pe.wait_ge(xT_lo_made, C * (b + 2))
                    for j in range(C):
                        pe.wait_ge(expo_made, C * (b + 2) + j - 1)
                        project(j, project_ps[j % 2])
                        turn(j)
                    for j, part in PHASE_ORDER_FIRST if first else PHASE_ORDER:
                        phase(j, part)
                else:
                    turn(1)
                    for j, part in PHASE_ORDER[:2]:
                        phase(j, part)
                    turn(2)
                    turn(3)
                    for j, part in PHASE_ORDER[2:]:
                        phase(j, part)

            step(0, True, first=True)
            with pe.Fori(1, NB - 1) as b:
                step(b, True)
            step(NB - 1, False)

        @block.vector
        def _(dve):
            dve.sem_inc(zT_made, TURN_CREDIT)
            tt, ts, stt = nc.vector.tensor_tensor, nc.vector.tensor_scalar, nc.vector.scalar_tensor_tensor

            def lower(dst, whole, hi):
                return tt(dst, whole, hi.bitcast(F32), ALU.subtract)

            def exponent(q, j, k, bank):
                dve.wait_ge(project_done, C * q + j + 1)
                stt(out=expo[:, j % 2, :], in0=norm_bc[:, k, :], scalar=neg_half_ab[:, j:j + 1],
                    in1=bank[:, :], op0=ALU.mult, op1=ALU.add).then_inc(expo_made, 1)

            def split_features(b, j):
                dve.wait_ge(exp_done, 2 * (C * (b + 1) + j + 1))
                lower(F_lo[:, j, :], F_raw[:, j % 2, :], F_hi[:, j, :]).then_inc(F_made, 1)

            def split_lo(b, c):
                dve.wait_ge(xT_hi_made, C * b + c + 1)
                lower(xT_lo[:, c, :], xT_raw[:, c, :], xT_hi[:, c, :]).then_inc(xT_lo_made, 1)

            for c in range(C):
                dve.wait_ge(gs_hi_made, c + 1)
                lower(gs_lo[:, c, :], trig[:, c, :], gs_hi[:, c, :]).then_inc(gs_lo_made, 1)
                dve.wait_ge(wT_hi_made, c + 1)
                lower(zT_lo[:, c, :], z[:, c, :], zT_hi[:, c, :]).then_inc(wT_lo_made, 1)
            dve.wait_ge(xis_loaded, 16)
            ts(neg_half_ab[:, :], ab[:, :], -0.5, None, ALU.mult).then_inc(half_ab_made, 1)
            for c in range(C):
                split_lo(0, c)
            dve.wait_ge(AB_made, 1)
            stt(out=W_scale[:, :], in0=AB[:, :], scalar=1.0 / R, in1=AB[:, :],
                op0=ALU.mult, op1=ALU.mult).then_inc(W_scale_made, 1)
            dve.wait_ge(half_ab_made, 1)
            dve.wait_ge(W_scale_made, 1)

            def scale_W(j):
                dve.wait_ge(W_hi_made, j + 1)
                stt(out=W_lo[:, j, :], in0=F_raw[:, j % 2, :], scalar=W_scale[:, j:j + 1],
                    in1=W_hi[:, j, :].bitcast(F32), op0=ALU.mult, op1=ALU.subtract).then_inc(W_made, 1)

            dve.wait_ge(norms_loaded, 16)
            exponent(0, 0, 0, token_ps[0])
            for j in range(1, C):
                exponent(0, j, 0, token_ps[j])
                scale_W(j - 1)
            dve.wait_ge(norms_loaded, 32)
            exponent(1, 0, 1, project_ps[0])
            scale_W(C - 1)
            for j in range(1, C):
                exponent(1, j, 1, (project_ps + turn_ps)[j])
                split_features(0, j - 1)
            split_features(0, C - 1)

            steps = 0
            def reduce_angles(buf, chunks, n, taken=False):
                nonlocal steps
                if taken:
                    for c in chunks:
                        dve.wait_ge(turns_made, n + c + 1)
                        stt(out=buf[:, c, :], in0=buf[:, C + c, :], scalar=TWO_PI_B / TWO_PI_A, in1=buf[:, c, :],
                            op0=ALU.mult, op1=ALU.add).then_inc(angle_step, 1)
                        steps += 1
                for part in () if taken else (TWO_PI_A, TWO_PI_B):
                    for i, c in enumerate(chunks):
                        if part == TWO_PI_A:
                            dve.wait_ge(turns_made, n + c + 1)
                        else:
                            dve.wait_ge(angle_step, steps - len(chunks) + 1)
                        stt(out=buf[:, c, :], in0=buf[:, C + c, :], scalar=-part, in1=buf[:, c, :],
                            op0=ALU.mult, op1=ALU.add).then_inc(angle_step, 1)
                        steps += 1
                for i, c in enumerate(chunks):
                    dve.wait_ge(angle_step, steps - len(chunks) + i + 1)
                    ts(buf[:, c, :], buf[:, c, :], PI_INSIDE, -PI_INSIDE, ALU.min, ALU.max).then_inc(angle_made, 1)

            def split_sine(buf, c, hi, lo, n, made):
                dve.wait_ge(sine_made, 2 * (n + c + 1))
                lower(lo[:, c, :], buf[:, C + c, :], hi[:, c, :]).then_inc(made, 1)

            for c in range(C):
                split_lo(1, c)
            reduce_angles(trig, (0, 1), 0)

            def halves(n, j, src, src_made, st, st_made):
                dve.wait_ge(src_made, n)
                nc.vector.bn_stats(st[:, j, :], src).then_inc(st_made, 1)

            def moments(j, st, m, m_made):
                nc.vector.bn_aggr(m[:, j, :], st[:, j, :]).then_inc(m_made, 1)

            def normalise(n, j, dst, src, root_made, m, root, dst_made):
                dve.wait_ge(root_made, n)
                ts(dst, src, m[:, j, 0:1], root[:, j:j + 1], ALU.subtract, ALU.mult).then_inc(dst_made, 1)

            def residual2(b, j):
                if j >= 2:
                    dve.wait_ge(out_made, C * b + j - 1)
                dve.wait_ge(mag_made, C * b + j + 1)
                tt(y2[:, j % 2, :], z[:, j, :], mag[:, j % 2, :], ALU.add).then_inc(y2_made, 1)
                halves(C * b + j + 1, j, y2[:, j % 2, :], y2_made, stats2, stats2_made)
                dve.wait_ge(stats2_made, C * b + j + 1)

            def norm2(b, j):
                dve.wait_ge(out_stored[j % 2], 32 * b + 16 * (j // 2) + STORE_CREDIT)
                normalise(C * b + j + 1, j, o_tile[:, j % 2, :], y2[:, j % 2, :], rstd2_made, mv2, rstd2, out_made)

            def step(b, pair, slot, more, ahead, first=False):
                n = [C * b + j + 1 for j in range(C)]
                dve.wait_ge(x_loaded[slot], 16 * (pair + 1 + slot))

                def residual1(j):
                    if j >= 2:
                        dve.wait_ge(z_made, n[j - 2])
                    dve.wait_ge(mix_done, n[j])
                    tt(y[:, j % 2, :], token_ps[j][:, :], x_tok[:, slot, j, :], ALU.add).then_inc(y_made, 1)

                def norm1(j):
                    normalise(n[j], j, z[:, j, :], y[:, j % 2, :], rstd_made, mv, rstd, z_made)

                def split_turned(j):
                    dve.wait_ge(zT_hi_made, n[j])
                    lower(zT_lo[:, j, :], turn_ps[j % 2][:, :], zT_hi[:, j, :]).then_inc(zT_made, 1)

                for j in range(C):
                    if j == 1:
                        dve.wait_ge(stats_made, n[0])
                    if not more and j == C - 1:
                        split_turned(0)
                    residual1(j)
                    if j == 0 and not first:
                        residual2(b - 1, C - 1)
                    if j == 1:
                        moments(0, stats, mv, mv_made)
                        if not first:
                            norm2(b - 1, C - 2)
                            moments(C - 1, stats2, mv2, mv2_made)
                    if first and j == C - 1:
                        dve.wait_ge(norms_loaded, 16 * (b + 3))
                        exponent(b + 2, 0, slot, project_ps[0])
                    halves(n[j], j, y[:, j % 2, :], y_made, stats, stats_made)
                    if j >= 1:
                        dve.wait_ge(stats_made, n[j])
                        norm1(j - 1)
                        moments(j, stats, mv, mv_made)
                    if j == 1 and not first:
                        norm2(b - 1, C - 1)
                    if more and not first and j == C - 1:
                        dve.wait_ge(norms_loaded, 16 * (b + 3))
                        exponent(b + 2, 0, slot, project_ps[0])
                if not more:
                    split_turned(1)
                norm1(C - 1)

                if first:
                    split_turned(0)
                    exponent(b + 2, 1, slot, project_ps[1])
                    reduce_angles(trig, (2, 3), 0, taken=True)
                    split_turned(1)
                    reduce_angles(late, (0,), C)
                    split_sine(trig, 2, cos_hi, cos_lo, 0, cos_made[1])
                    split_sine(trig, 3, cos_hi, cos_lo, 0, cos_made[1])
                    split_turned(2)
                    reduce_angles(late, (1,), C)
                    reduce_angles(late, (2, 3), C, taken=True)
                    split_turned(3)
                    split_sine(late, 2, sin_hi, sin_lo, C, sin_made[1])
                    split_sine(late, 3, sin_hi, sin_lo, C, sin_made[1])
                    split_features(b + 1, 0)
                    exponent(b + 2, 2, slot, project_ps[0])
                    split_features(b + 1, 1)
                    exponent(b + 2, 3, slot, project_ps[1])
                    split_features(b + 1, 2)
                    split_features(b + 1, 3)
                else:
                    for j in range(C):
                        if more and j >= 1:
                            exponent(b + 2, j, slot, project_ps[j % 2])
                        if more or j >= 2:
                            split_turned(j)
                        if more:
                            split_features(b + 1, j)

                def add_squares(j):
                    dve.wait_ge(square_done, 2 * C * b + 2 * j + 2 + SQUARE_CREDIT)
                    tt(re2[:, j % 2, :], re2[:, j % 2, :], im2[:, j % 2, :], ALU.add).then_inc(sum_made, 1)

                if first:
                    add_squares(0)
                    add_squares(1)
                for j in range(C):
                    if j >= 1:
                        residual2(b, j - 1)
                    if ahead:
                        split_lo(b + 2, j)
                    if j >= 1:
                        moments(j - 1, stats2, mv2, mv2_made)
                    if j >= 2:
                        norm2(b, j - 2)
                    if not (first and j < 2):
                        add_squares(j)

            step(0, 0, 0, True, True, first=True)
            step(1, 0, 1, True, True)
            with dve.Fori(1, NB // 2 - 1) as pair:
                for slot in range(2):
                    step(pair * 2 + slot, pair, slot, True, True)
            step(NB - 2, NB // 2 - 1, 0, True, False)
            step(NB - 1, NB // 2 - 1, 1, False, False)
            residual2(NB - 1, C - 1)
            moments(C - 1, stats2, mv2, mv2_made)
            norm2(NB - 1, C - 2)
            norm2(NB - 1, C - 1)


def kernel(**inputs):
    import concourse.bacc as _bacc
    from concourse.bass_utils import run_bass_kernel_spmd as _run

    x = np.asarray(inputs["L0_attn_x"])
    tokens = x.reshape(-1, x.shape[-1])
    w = np.asarray(inputs["L0_attn_input_weights"])
    gs = np.asarray(inputs["L0_attn_proj_matrix"])
    laid = {
        "xT": tokens.T, "x": tokens, "wT": w.T, "w": w, "xis": inputs["L0_attn_xis"], "gsT": gs.T,
        "theta": inputs["L0_ffn_theta"], "phi": inputs["L0_ffn_phi"],
        "theta_noise": inputs["L0_ffn_theta_noise"], "phi_noise": inputs["L0_ffn_phi_noise"],
    }
    nc = _bacc.Bacc("TRN2", target_bir_lowering=False, num_devices=1)
    arrays, args = {}, []
    for name, a in laid.items():
        a = np.ascontiguousarray(a)
        arrays[f"in_{name}"] = a
        args.append(nc.dram_tensor(f"in_{name}", a.shape, mybir.dt.from_np(a.dtype), kind="ExternalInput").ap())
    args.append(nc.dram_tensor("out_tokens", tokens.shape, F32, kind="ExternalOutput").ap())
    build(nc, *args)
    r = _run(nc, [arrays], core_ids=[0])
    return r.results[0]["out_tokens"].reshape(x.shape)
```
